# Optimizing a Trainium2 kernel written in Bass

```python
import numpy as np
import jax
import jax.numpy as jnp

def _softmax(x, axis=-1):
    return jax.nn.softmax(x, axis=axis)

def _gelu(x):
    return jax.nn.gelu(x, approximate=True)

def _silu(x):
    return jax.nn.silu(x)

def _sigmoid(x):
    return jax.nn.sigmoid(x)

def _layernorm(x, axis=-1, eps=1e-05):
    m = jnp.mean(x, axis=axis, keepdims=True)
    v = jnp.var(x, axis=axis, keepdims=True)
    return (x - m) / jnp.sqrt(v + eps)

def _scatter_add(tgt, idx, src, axis=0):
    return tgt.at[idx].add(src)

def _segment_sum(src, seg, n):
    return jax.ops.segment_sum(src, seg, n)
kernel_name = 'mk_gnn_ffn_d1_gnn_r8_890b99'

def setup_inputs(seed: int=0):
    np.random.seed(seed)
    _w = jnp.asarray

    def _rec_inputs():
        import jax
        import jax.numpy as jnp
        _gk = jax.random.key(seed)
        x = -7.329e-05 + 0.9999 * jax.random.normal(jax.random.fold_in(_gk, 1), (12500, 256), jnp.float32)
        src = jax.random.randint(jax.random.fold_in(_gk, 2), (200000,), 0, 12500, jnp.int32)
        dst = jnp.minimum((12500 * jax.random.uniform(jax.random.fold_in(_gk, 3), (200000,)) ** 2.0).astype(jnp.int32), 99999)
        _o = jnp.argsort(dst, stable=True)
        src = src[_o]
        dst = dst[_o]
        return (x, src, dst)
    x, src, dst = _rec_inputs()

    def _L0_gnn_setup():
        import jax, jax.numpy as jnp
        import numpy as np
        N = 25000
        E = 75000
        C = 256
        key = jax.random.key(seed)
        k1, k2, k3, k4, k5 = jax.random.split(key, 5)
        x = jax.random.normal(k1, (N, C), dtype=jnp.float32)
        sources = jax.random.randint(k2, (E,), 0, N, dtype=jnp.int64)
        targets = jax.random.randint(k3, (E,), 0, N, dtype=jnp.int64)
        norm = jax.random.uniform(k4, (N, 1), dtype=jnp.float32)
        std = float(np.sqrt(2.0 / (C + C)))
        weight = jax.random.normal(k5, (C, C), dtype=jnp.float32) * std
        return {'x': x, 'sources': sources, 'targets': targets, 'norm': norm, 'weight': weight}
    _L0_gnn_all = _L0_gnn_setup()
    _L0_gnn_in = {k: v for k, v in _L0_gnn_all.items() if k in ('weight',)}
    del _L0_gnn_all

    def _L0_ffn_setup():
        import jax, jax.numpy as jnp
        import numpy as np
        C = 256
        HID = 1024
        E = 8
        TEMP = 1.0
        key = jax.random.key(seed)
        ks = jax.random.split(key, 7)
        x = jax.random.normal(ks[0], (8, 2048, C), dtype=jnp.float32)
        W1 = jax.random.normal(ks[1], (C, HID), dtype=jnp.float32) * 0.02
        b1 = jnp.zeros((HID,), dtype=jnp.float32)
        Wg = jax.random.normal(ks[2], (HID, E), dtype=jnp.float32) * 0.02
        bg = jnp.zeros((E,), dtype=jnp.float32)
        Wd = jax.random.normal(ks[3], (E, HID, C), dtype=jnp.float32) * 0.02
        bd = jnp.zeros((E, C), dtype=jnp.float32)
        return {'x': x, 'W1': W1, 'b1': b1, 'Wg': Wg, 'bg': bg, 'Wd': Wd, 'bd': bd}
    _L0_ffn_all = _L0_ffn_setup()
    _L0_ffn_in = {k: v for k, v in _L0_ffn_all.items() if k in ('W1', 'b1', 'Wg', 'bg', 'Wd', 'bd')}
    del _L0_ffn_all
    return {'x': x, 'src': src, 'dst': dst, 'L0_gnn_weight': _L0_gnn_in['weight'], 'L0_ffn_W1': _L0_ffn_in['W1'], 'L0_ffn_b1': _L0_ffn_in['b1'], 'L0_ffn_Wg': _L0_ffn_in['Wg'], 'L0_ffn_bg': _L0_ffn_in['bg'], 'L0_ffn_Wd': _L0_ffn_in['Wd'], 'L0_ffn_bd': _L0_ffn_in['bd']}

def reference(x, src, dst, L0_gnn_weight, L0_ffn_W1, L0_ffn_b1, L0_ffn_Wg, L0_ffn_bg, L0_ffn_Wd, L0_ffn_bd):
    import jax
    import jax.numpy as jnp

    def _L0_gnn_ref(x, sources, targets, norm, weight):
        import jax, jax.numpy as jnp
        import numpy as np
        N = 25000
        E = 75000
        C = 256
        agg = x.at[targets].add(x[sources])
        h = norm * agg
        return h @ weight

    def _L0_ffn_ref(x, W1, b1, Wg, bg, Wd, bd):
        import jax, jax.numpy as jnp
        import numpy as np
        C = 256
        HID = 1024
        E = 8
        TEMP = 1.0
        orig_shape = x.shape
        xf = x.reshape(-1, orig_shape[-1])
        H = jax.nn.gelu(xf @ W1 + b1, approximate=False)
        probs = jax.nn.softmax((H @ Wg + bg) / TEMP, axis=-1)
        assign = jnp.argmax(probs, axis=-1)
        out = jnp.zeros_like(xf)
        for e in range(Wd.shape[0]):
            y = H @ Wd[e] + bd[e]
            sel = (assign == e)[:, None]
            out = out + jnp.where(sel, probs[:, e:e + 1] * y, 0.0)
        return out.reshape(orig_shape)
    deg = jnp.maximum(jax.ops.segment_sum(jnp.ones(dst.shape, jnp.float32), dst, num_segments=12500), 1.0)
    deg_isqrt = deg ** (-0.5)
    x = x + _L0_gnn_ref(_layernorm(x, axis=-1), src, dst, deg_isqrt[:, None], L0_gnn_weight)
    x = x + _L0_ffn_ref(_layernorm(x, axis=-1)[None], L0_ffn_W1, L0_ffn_b1, L0_ffn_Wg, L0_ffn_bg, L0_ffn_Wd, L0_ffn_bd)[0]
    return x

_drawn_inputs = setup_inputs


def setup_inputs(seed=0):
    import zlib

    import numpy as np

    out = dict(_drawn_inputs(seed))
    spreads = {'L0_ffn_b1': (0.0, 0.8), 'L0_ffn_bg': (0.0, 0.571), 'L0_ffn_bd': (0.0, 0.8)}
    factors = {'L0_ffn_W1': 3.841, 'L0_ffn_Wg': 4.103, 'L0_ffn_Wd': 4.712}
    for name, (base, spread) in spreads.items():
        noise = np.random.default_rng([zlib.crc32(name.encode()), seed]).standard_normal(out[name].shape)
        drawn = base * np.exp(spread * noise) if base else spread * noise
        out[name] = jnp.asarray(drawn.astype(out[name].dtype))
    for name, factor in factors.items():
        out[name] = (out[name] * factor).astype(out[name].dtype)
    return out
```

```python
import concourse.bass as bass
from concourse import mybir
from contextlib import ExitStack


def gnn_moe_program(nc, x, src, dst, w_gnn, w1, b1, wg, bg, wd, bd, out):
    F32, I32, U32 = mybir.dt.float32, mybir.dt.int32, mybir.dt.uint32
    ALU = mybir.AluOpType
    ACT = mybir.ActivationFunctionType
    AX = mybir.AxisListType

    P = 128
    N, C = x.shape
    E = src.shape[0]
    HID = w1.shape[1]
    NE = wg.shape[1]
    EPS = 1e-5
    KC = C // P
    KH = HID // P
    NT = -(-N // P)
    LAST = N - (NT - 1) * P
    NPAD = NT * P
    LN_GROUPS = 7
    LT = NT // LN_GROUPS
    assert NT % LN_GROUPS == 0 and NT % 2 == 0
    U = 4
    RING = 4
    NB = -(-E // (U * P * RING)) * RING
    NCH = NB * U
    AGG_ITERS = NB // RING
    CROWS = -(-NCH // P)
    BROWS = -(-NB // P)
    PAD_DST = NPAD - 1
    assert N <= PAD_DST
    AW = C + 1
    BT = 2 * P
    SUPER = NT // 2
    CAP = NPAD + BT
    QMAX = (NPAD // BT + NE + 1) // 2 * 2
    G5 = 7
    N5 = NT // (2 * G5)
    assert NT == N5 * 2 * G5

    ctx = ExitStack()
    with ctx:
        def sb(name, shape, dt=F32):
            return ctx.enter_context(nc.sbuf_tensor(name, shape, dt))

        def pb(name):
            return ctx.enter_context(nc.psum_tensor(name, [P, 512], F32))

        def sem(name):
            return ctx.enter_context(nc.semaphore(name))

        table = nc.dram_tensor("xn_table", (NPAD, C), F32).ap()
        ranges_d = nc.dram_tensor("tile_ranges", (2 * BROWS, P), I32).ap()
        y_rows = nc.dram_tensor("y_rows", (QMAX * BT, C), F32).ap()
        routed = nc.dram_tensor("routed_rows", (NE * CAP + 2 * BT, C), F32).ap()

        agg = sb("agg", [P, NT, AW])
        dst_t = sb("dst_t", [P, NCH])
        src_t = sb("src_t", [P, NCH], I32)
        gath = sb("gath", [P, RING * U, 260])
        onehot = sb("onehot", [P, RING * U, P])
        idx_ring = sb("idx_ring", [P, RING * U], U32)
        ranges = sb("ranges", [1, 2 * BROWS * P], I32)
        iota = sb("iota", [P, P])
        ident = sb("ident", [P, P])
        before = sb("before", [P, P])
        ones = sb("ones", [P, P])
        tile_base = sb("tile_base", [P, NT])
        iota8 = sb("iota8", [P, NE])
        w_sb = sb("w_sb", [P, KC, C])
        w1_sb = sb("w1_sb", [P, KC, HID])
        b1_sb = sb("b1_sb", [P, KH])
        wg_sb = sb("wg_sb", [P, KH, NE])
        bg_sb = sb("bg_sb", [NE, 1])
        wd_sb = sb("wd_sb", [P, 2, KH, C])
        bd_sb = sb("bd_sb", [P, 2, C])
        hid = sb("hid", [P, KH, BT])
        rows_t = sb("rows_t", [P, KC, BT])
        rows = sb("rows", [P, 2, C])
        agg_t = sb("agg_t", [P, KC, BT])
        xraw = sb("xraw", [P, 2, C])
        yrow = sb("yrow", [P, 2, C])
        zrow = sb("zrow", [P, 2, C])
        stats = sb("stats", [P, LT, 6])
        mv = sb("mv", [P, LT, 2])
        rstd = sb("rstd", [P, NT])
        norm = sb("norm", [P, NT])
        deg = sb("deg", [P, NT])
        nr_a = sb("nr_a", [P, NT])
        nr_b = sb("nr_b", [P, NT])
        nr_i = sb("nr_i", [P, NT], I32)
        logit_t = sb("logit_t", [NE, BT])
        logit = sb("logit", [P, 2, NE])
        max8 = sb("max8", [P, 2, 8])
        arg8 = sb("arg8", [P, 2, 8], U32)
        argf = sb("argf", [P, 2])
        pick = sb("pick", [P, 2, NE])
        place = sb("place", [P, 2, NE])
        base = sb("base", [P, NE])
        posf = sb("posf", [P, 2])
        pos_now = sb("pos_now", [P, 2], U32)
        pos_all = sb("pos_all", [P, NT])
        arg_all = sb("arg_all", [P, NT])
        below_max = sb("below_max", [P, NT, NE])
        prob = sb("prob", [P, NT])
        pos_ring = sb("pos_ring", [P, 2 * G5], U32)
        cnt = sb("cnt", [P, NE])
        cnt_i = sb("cnt_i", [P, NE], I32)
        cum = sb("cum", [P, NE + 2])
        shift = sb("shift", [P, NE])
        zero_at = sb("zero_at", [1, NE], I32)
        q_iota = sb("q_iota", [1, QMAX])
        q_e = sb("q_e", [1, QMAX])
        q_row = sb("q_row", [1, QMAX])
        q_lo = sb("q_lo", [1, QMAX])
        q_hi = sb("q_hi", [1, QMAX])
        q_tab = sb("q_tab", [1, 2, QMAX], I32)
        q_n = sb("q_n", [1, 1], I32)

        spare = gath[:, :, :].rearrange("p a b -> p (a b)")
        dst_i = spare[:, 0:CROWS * P].bitcast(I32)
        src_i = spare[:, CROWS * P:2 * CROWS * P].bitcast(I32)
        spare2 = onehot[:, :, :].rearrange("p a b -> p (a b)")
        blk_i = spare2.bitcast(I32)
        dst_f = wd_sb[:, :, :, :].rearrange("p a b c -> p (a b c)")[:, 0:CROWS * P]
        src_f = wd_sb[:, :, :, :].rearrange("p a b c -> p (a b c)")[:, CROWS * P:2 * CROWS * P]
        blk_lo = nr_i[:, 0:BROWS]
        blk_hi = nr_i[:, BROWS:2 * BROWS]
        blk_f = nr_a[:, 0:2 * BROWS]
        range_f = rows[0:2 * BROWS, 0, 0:P]
        range_i = rows[0:2 * BROWS, 1, 0:P].bitcast(I32)

        ps_agg = [pb(f"ps_agg{r}") for r in range(RING)]
        ps_t = pb("ps_t")
        ps_m = pb("ps_m")
        ps_h = [pb(f"ps_h{i}") for i in range(2)]
        ps_gate, ps_small = ps_agg[0], ps_agg[1]

        names = """pads_set edges_in weights_in const_base consts_ready edges_float tr_done dst_copied src_copied
        blk_ready blk_tr blk_rows range_out range_in normed table_written
        idx_ready gather_turn sp_turn onehot_ready sums_done sums_added sums_final
        agg_ready xraw0_in xraw1_in aggt_done aggt_copied gnn_done x1_done rows_ready rowst_done rowst_copied
        hid_done gelu_done gate_done gate_copied gatet_done pick_ready place_done pos_ready
        scat_done zero_ready tail_zeroed plan_ready blk_in wd_in0 wd_in1
        y_done y_ready y_stored prob_ready pos_put exp_done t_turn out_done0 out_done1 out_ready zeros_in spare_zeroed""".split()
        s = {n: sem(n) for n in names}
        x_in = [sem(f"x_in{g}") for g in range(LN_GROUPS)]
        gathered = [sem(f"gathered{r}") for r in range(RING)]
        visit_done = [sem(f"visit_done{r}") for r in range(RING)]
        y_in = [sem(f"y_in{i}") for i in range(2 * G5)]

        block = ctx.enter_context(nc.Block())

        def edge_rows(a):
            def pieces(w, ncol):
                full = E // (P * w)
                yield (slice(0, P), slice(0, full), a[0:full * P * w].rearrange("(j p q) -> p j q", p=P, q=w))
                rest = E - full * P * w
                n = rest // w
                yield (slice(0, n), full, a[full * P * w:full * P * w + n * w].rearrange("(p q) -> p q", q=w))
                if rest % w:
                    yield (slice(n, n + 1), full, a[E - rest % w:E].rearrange("(p q) -> p q", p=1))
            return pieces

        def load_edges(eng, a, buf, w):
            n = 0
            for p, j, part in edge_rows(a)(w, None):
                d = buf[p, j, 0:part.shape[-1]]
                eng.dma_start(d, part).then_inc(s["edges_in"], 16)
                n += 16
            return n

        CH_PIECES = 3 if (E % (P * P)) % P else 2
        BL_PIECES = 3 if (E % (P * U * P)) % (U * P) else 2

        @block.sync
        def _(sp):
            sp.wait_ge(s["pads_set"], 1)
            for g in range(LN_GROUPS):
                t0, t1 = g * LT, (g + 1) * LT
                full = t1 if t1 < NT else NT - 1
                sp.dma_start(agg[:, t0:full, 0:C],
                             x[t0 * P:full * P, :].rearrange("(t p) c -> p t c", p=P)).then_inc(x_in[g], 16)
                if full < t1:
                    sp.dma_start(agg[0:LAST, NT - 1, 0:C], x[(NT - 1) * P:N, :]).then_inc(x_in[g], 16)
                if g == 0:
                    load_edges(sp, dst, dst_i.rearrange("p (j q) -> p j q", q=P), P)
                    load_edges(sp, src, src_i.rearrange("p (j q) -> p j q", q=P), P)
                    load_edges(sp, dst, blk_i.rearrange("p (j q) -> p j q", q=U * P), U * P)
            sp.dma_start(w_sb[:, :, :], w_gnn.rearrange("(k p) c -> p k c", p=P)).then_inc(s["weights_in"], 16)
            sp.dma_start(w1_sb[:, :, :], w1.rearrange("(k p) c -> p k c", p=P)).then_inc(s["weights_in"], 16)
            sp.dma_start(wg_sb[:, :, :], wg.rearrange("(k p) c -> p k c", p=P)).then_inc(s["weights_in"], 16)
            with nc.allow_non_contiguous_dma(reason="a few bias values"):
                sp.dma_start(b1_sb[:, :], b1.rearrange("(k p) -> p k", p=P)).then_inc(s["weights_in"], 16)
                sp.dma_start(bg_sb[:, :], bg.rearrange("(p q) -> p q", q=1)).then_inc(s["weights_in"], 16)
            sp.wait_ge(s["blk_rows"], 1)
            sp.dma_start(ranges_d, range_i).then_inc(s["range_out"], 16)
            sp.wait_ge(s["range_out"], 16)
            sp.dma_start(ranges[0:1, :], ranges_d.rearrange("(o a) q -> o (a q)", o=1)).then_inc(s["range_in"], 16)
            for g in range(LN_GROUPS):
                sp.wait_ge(s["normed"], g + 1)
                sp.dma_start(table[g * LT * P:(g + 1) * LT * P, :].rearrange("(t p) c -> p t c", p=P),
                             agg[:, g * LT:(g + 1) * LT, 0:C]).then_inc(s["table_written"], 16)
            sp.wait_ge(s["zero_ready"], 1)
            sp.dma_start(routed[NE * CAP:NE * CAP + 2 * BT, :].rearrange("(a p k) c -> p a (k c)", a=2, p=P),
                         zrow[:, :, :].rearrange("p k c -> p (k c)").unsqueeze(1).to_broadcast([P, 2, 2 * C])
                         ).then_inc(s["spare_zeroed"], 16)
            for q in range(SUPER, QMAX):
                sp.dma_start(y_rows[q * BT:(q + 1) * BT, :].rearrange("(p k) c -> p k c", p=P), zrow[:, :, :]
                             ).then_inc(s["spare_zeroed"], 16)
            with sp.Fori(0, SUPER - 1) as i:
                sp.wait_ge(s["x1_done"], i)
                sp.sem_inc(s["sp_turn"], 1)
                sp.dma_start(xraw[:, 0, :], x[bass.ds(i * BT, P), :]).then_inc(s["xraw0_in"], 16)
                sp.dma_start(xraw[:, 1, :], x[bass.ds(i * BT + P, P), :]).then_inc(s["xraw1_in"], 16)
            sp.wait_ge(s["x1_done"], SUPER - 1)
            sp.dma_start(xraw[:, 0, :], x[(NT - 2) * P:(NT - 1) * P, :]).then_inc(s["xraw0_in"], 16)
            sp.dma_start(xraw[0:LAST, 1, :], x[(NT - 1) * P:N, :]).then_inc(s["xraw1_in"], 16)
            sp.wait_ge(s["plan_ready"], 1)
            for e in range(NE):
                at = sp.value_load(zero_at[0:1, e:e + 1], min_val=0, max_val=NE * CAP)
                sp.dma_start(routed[bass.ds(at, BT), :].rearrange("(p k) c -> p k c", p=P),
                             zrow[:, :, :]).then_inc(s["tail_zeroed"], 16)
            sp.wait_ge(s["tail_zeroed"], NE * 16)
            sp.wait_ge(s["scat_done"], SUPER * 32)
            sp.wait_ge(s["spare_zeroed"], 16 * (1 + QMAX - SUPER))
            steps = sp.value_load(q_n[0:1, 0:1], min_val=1, max_val=QMAX // 2)
            with sp.Fori(0, steps) as i:
                for h in range(2):
                    e = sp.value_load(q_tab[0:1, 0, bass.ds(2 * i + h, 1)], min_val=0, max_val=NE - 1)
                    row = sp.value_load(q_tab[0:1, 1, bass.ds(2 * i + h, 1)], min_val=0, max_val=NE * CAP + BT)
                    sp.wait_ge(s["y_ready"], 2 * i + h)
                    sp.sem_inc(s["sp_turn"], 1)
                    sp.dma_start(rows[:, :, :], routed[bass.ds(row, BT), :].rearrange("(p k) c -> p k c", p=P)
                                 ).then_inc(s["blk_in"], 16)
                    sp.dma_start(wd_sb[:, h, :, :],
                                 wd[bass.ds(e, 1), :, :].rearrange("o (k p) c -> p (o k) c", p=P)
                                 ).then_inc(s[f"wd_in{h}"], 16)
                    sp.dma_start(bd_sb[:, h, :], bd[bass.ds(e, 1), :].to_broadcast([P, C])).then_inc(s[f"wd_in{h}"], 16)
                    sp.wait_ge(s["y_ready"], 2 * i + h + 1)
                    sp.sem_inc(s["sp_turn"], 1)
                    sp.dma_start(y_rows[bass.ds((2 * i + h) * BT, BT), :].rearrange("(p k) c -> p k c", p=P),
                                 yrow[:, :, :]).then_inc(s["y_stored"], 16)
                    sp.wait_ge(s["y_stored"], 32 * i + 16 * h + 16)
                    sp.sem_inc(s["sp_turn"], 1)
            sp.sem_inc(s["blk_ready"], 1)
            with sp.Fori(0, N5 - 1) as i:
                for h in range(2):
                    sp.wait_ge(s["out_ready"], 2 * i + h + 1)
                    sp.sem_inc(s["sp_turn"], 1)
                    sp.dma_start(out[bass.ds((2 * i + h) * (G5 * P), G5 * P), :].rearrange("(t p) c -> p t c", p=P),
                                 gath[:, h * G5:(h + 1) * G5, 0:C]).then_inc(s[f"out_done{h}"], 16)
            sp.wait_ge(s["out_ready"], 2 * N5 - 1)
            t0 = (2 * N5 - 2) * G5
            sp.dma_start(out[t0 * P:(t0 + G5) * P, :].rearrange("(t p) c -> p t c", p=P),
                         gath[:, 0:G5, 0:C]).then_inc(s["out_done0"], 16)
            t0 += G5
            sp.wait_ge(s["out_ready"], 2 * N5)
            sp.dma_start(out[t0 * P:(NT - 1) * P, :].rearrange("(t p) c -> p t c", p=P),
                         gath[:, G5:2 * G5 - 1, 0:C]).then_inc(s["out_done1"], 16)
            sp.dma_start(out[(NT - 1) * P:N, :], gath[0:LAST, 2 * G5 - 1, 0:C]).then_inc(s["out_done1"], 16)
            sp.wait_ge(s["out_done0"], 16 * N5)
            sp.wait_ge(s["out_done1"], 16 * (N5 + 1))

        @block.gpsimd
        def _(pool):
            pool.memset(ident[:, :], 0.0).then_inc(s["const_base"], 1)
            pool.memset(before[:, :], 1.0).then_inc(s["const_base"], 1)
            pool.iota(iota[:, :], pattern=[[1, P]], base=0, channel_multiplier=0,
                      allow_small_or_imprecise_dtypes=True).then_inc(s["consts_ready"], 1)
            pool.iota(tile_base[:, :], pattern=[[P, NT]], base=0, channel_multiplier=0,
                      allow_small_or_imprecise_dtypes=True).then_inc(s["consts_ready"], 1)
            pool.iota(iota8[:, :], pattern=[[1, NE]], base=0, channel_multiplier=0,
                      allow_small_or_imprecise_dtypes=True).then_inc(s["consts_ready"], 1)
            pool.iota(base[:, :], pattern=[[CAP, NE]], base=0, channel_multiplier=0,
                      allow_small_or_imprecise_dtypes=True).then_inc(s["consts_ready"], 1)
            pool.iota(q_iota[:, :], pattern=[[1, QMAX]], base=0, channel_multiplier=0,
                      allow_small_or_imprecise_dtypes=True).then_inc(s["consts_ready"], 1)
            pool.wait_ge(s["const_base"], 2)
            pool.affine_select(out=ident[:, :], in_=ident[:, :], compare_op=ALU.not_equal, fill=1.0, base=0,
                               pattern=[[-1, P]], channel_multiplier=1).then_inc(s["consts_ready"], 1)
            pool.affine_select(out=before[:, :], in_=before[:, :], compare_op=ALU.is_gt, fill=0.0, base=0,
                               pattern=[[1, P]], channel_multiplier=-1).then_inc(s["consts_ready"], 1)
            pool.wait_ge(s["table_written"], 16 * LN_GROUPS)
            with pool.Fori(0, AGG_ITERS) as i:
                for r in range(RING):
                    pool.wait_ge(s["sums_done"], RING * i + r + 1)
                    pool.wait_ge(s["idx_ready"], RING * i + r + 1)
                    pool.sem_inc(s["gather_turn"], 1)
                    for u in range(U):
                        k = r * U + u
                        pool.indirect_dma_start(
                            gath[:, k, 0:C], None, table,
                            bass.IndirectOffsetOnAxis(ap=idx_ring[:, k:k + 1], axis=0)).then_inc(gathered[r], 16)
            with pool.Fori(0, SUPER) as i:
                pool.wait_ge(s["pos_ready"], i + 1)
                pool.sem_inc(s["gather_turn"], 1)
                for a in range(2):
                    pool.indirect_dma_start(
                        routed, bass.IndirectOffsetOnAxis(ap=pos_now[:, a:a + 1], axis=0),
                        rows[:, a, :], None).then_inc(s["scat_done"], 16)
            pool.wait_ge(s["blk_ready"], 1)
            with pool.Fori(0, N5) as i:
                for h in range(2):
                    pool.wait_ge(s["pos_put"], 2 * i + h + 1)
                    pool.sem_inc(s["gather_turn"], 1)
                    for u in range(G5):
                        k = h * G5 + u
                        pool.indirect_dma_start(
                            gath[:, k, 0:C], None, y_rows,
                            bass.IndirectOffsetOnAxis(ap=pos_ring[:, k:k + 1], axis=0)).then_inc(y_in[k], 16)

        @block.scalar
        def _(act):
            act.preload_act_table(ACT.Gelu)
            for j in range(0, CROWS, 4):
                m = min(4 * P, NCH - j * P)
                g = j // 4
                act.wait_ge(s["tr_done"], 2 * g + 2)
                act.copy(src_t[:, j * P:j * P + m], ps_m[:, 0:m] if g % 2 == 0 else ps_h[1][:, 0:m]
                         ).then_inc(s["src_copied"], 1)
            act.drain()
            with act.Fori(0, AGG_ITERS) as i:
                for r in range(RING):
                    act.wait_ge(gathered[r], i * (16 * U))
                    act.copy(idx_ring[:, r * U:(r + 1) * U],
                             src_t[:, bass.ds(i * (RING * U) + r * U, U)]).then_inc(s["idx_ready"], 1)

            def hidden(first):
                for k in range(KH):
                    act.wait_ge(s["hid_done"], first + k + 1)
                    act.activation(hid[:, k, :], ps_h[k % 2][:, 0:BT], ACT.Gelu,
                                   bias=b1_sb[:, k:k + 1]).then_inc(s["gelu_done"], 1)

            act.wait_ge(s["weights_in"], 80)
            with act.Fori(0, SUPER) as i:
                act.wait_ge(s["gate_done"], i)
                hidden(KH * i)
            act.wait_ge(s["plan_ready"], 1)
            steps = act.value_load(q_n[0:1, 0:1], min_val=1, max_val=QMAX // 2)
            with act.Fori(0, steps) as i:
                for h in range(2):
                    act.wait_ge(s["y_done"], 2 * i + h)
                    hidden(KH * SUPER + KH * (2 * i + h))
            act.wait_ge(s["blk_ready"], 1)
            act.activation(below_max[:, :, :], below_max[:, :, :], ACT.Exp).then_inc(s["exp_done"], 1)

        @block.vector
        def _(dve):
            def rsqrt(y, v, n):
                a, b, i = nr_a[:, 0:n], nr_b[:, 0:n], nr_i[:, 0:n]
                dve.tensor_scalar(i, v.bitcast(I32), 1, None, ALU.logical_shift_right)
                dve.tensor_scalar(a, v, -0.5, None, ALU.mult)
                dve.drain()
                dve.tensor_scalar(i, i, -1.0, float(0x5F3759DF), ALU.mult, ALU.add)
                dve.drain()
                guess = i.bitcast(F32)
                for step in range(4):
                    old = guess if step == 0 else y
                    dve.tensor_tensor(b, old, old, ALU.mult)
                    dve.drain()
                    dve.tensor_tensor(b, b, a, ALU.mult)
                    dve.drain()
                    dve.scalar_tensor_tensor(y, b, 1.5, old, ALU.add, ALU.mult)
                    dve.drain()

            dve.memset(agg[:, NT - 1, :], 0.0)
            dve.memset(dst_i, PAD_DST)
            dve.memset(src_i, 0)
            dve.memset(blk_i, PAD_DST)
            dve.memset(zrow[:, :, :], 0.0).then_inc(s["zero_ready"], 1)
            dve.memset(xraw[:, :, :], 0.0)
            dve.memset(ones[:, :], 1.0)
            dve.drain()
            dve.sem_inc(s["pads_set"], 1)
            dve.wait_ge(s["edges_in"], 16 * (2 * CH_PIECES + BL_PIECES))
            dve.tensor_copy(dst_f, dst_i).then_inc(s["edges_float"], 1)
            dve.tensor_copy(src_f, src_i).then_inc(s["edges_float"], 1)
            bl = blk_i.rearrange("p (j q) -> p j q", q=U * P)
            dve.tensor_reduce(blk_lo, bl, AX.X, ALU.min)
            dve.tensor_reduce(blk_hi, bl, AX.X, ALU.max)
            dve.drain()
            dve.tensor_scalar(nr_i[:, 0:2 * BROWS], nr_i[:, 0:2 * BROWS], P.bit_length() - 1, None,
                              ALU.arith_shift_right)
            dve.drain()
            dve.tensor_copy(blk_f, nr_i[:, 0:2 * BROWS]).then_inc(s["blk_ready"], 1)
            for j in range(0, CROWS, 4):
                m = min(4 * P, NCH - j * P)
                g = j // 4
                dve.wait_ge(s["tr_done"], 2 * g + 1)
                dve.tensor_copy(dst_t[:, j * P:j * P + m], ps_t[:, 0:m] if g % 2 == 0 else ps_h[0][:, 0:m]
                                ).then_inc(s["dst_copied"], 1)
            dve.wait_ge(s["blk_tr"], 1)
            dve.tensor_copy(range_f, ps_agg[0][0:2 * BROWS, 0:P])
            dve.drain()
            dve.tensor_copy(range_i, range_f).then_inc(s["blk_rows"], 1)
            for g in range(LN_GROUPS):
                dve.wait_ge(x_in[g], 32 if g == LN_GROUPS - 1 else 16)
                with dve.Fori(0, LT) as t:
                    dve.bn_stats(stats[:, bass.ds(t, 1), :].rearrange("p a b -> p (a b)"),
                                 agg[:, bass.ds(t + g * LT, 1), 0:C].rearrange("p a b -> p (a b)"))
                dve.drain()
                for t in range(LT):
                    dve.bn_aggr(mv[:, t, :], stats[:, t, :])
                dve.drain()
                dve.tensor_scalar(deg[:, 0:LT], mv[:, :, 1], EPS, None, ALU.add)
                dve.drain()
                rsqrt(rstd[:, 0:LT], deg[:, 0:LT], LT)
                with dve.Fori(0, LT) as t:
                    row = agg[:, bass.ds(t + g * LT, 1), 0:C].rearrange("p a b -> p (a b)")
                    dve.tensor_scalar(row, row, mv[:, bass.ds(t, 1), 0], rstd[:, bass.ds(t, 1)],
                                      ALU.subtract, ALU.mult)
                dve.drain()
                dve.sem_inc(s["normed"], 1)
            dve.memset(agg[:, :, C], 0.0)
            dve.memset(gath[:, :, C], 1.0)
            dve.drain()
            dve.wait_ge(s["consts_ready"], 7)
            dve.wait_ge(s["range_in"], 16)
            dve.sem_inc(s["sums_done"], RING)

            made = [dve.alloc_register(f"made{r}") for r in range(RING)]
            for r in range(RING):
                dve.reg_mov(made[r], 0)

            def make_onehot(i, r, t):
                before_this = dve.snap(made[r])
                dve.wait_ge(visit_done[r], before_this)
                for u in range(U):
                    k = r * U + u
                    q = dve.tensor_scalar(onehot[:, k, :], iota[:, :], tile_base[:, bass.ds(t, 1)],
                                          dst_t[:, bass.ds(i * (RING * U) + k, 1)], ALU.add, ALU.is_equal)
                q.then_inc(s["onehot_ready"], 1)
                dve.reg_add(made[r], made[r], 1)

            def add_sums(r, t):
                n = dve.snap(made[r])
                dve.wait_ge(visit_done[r], n)
                row = agg[:, bass.ds(t, 1), :].rearrange("p a b -> p (a b)")
                dve.tensor_tensor(row, row, ps_agg[r][:, 0:AW], ALU.add)
                dve.drain()
                dve.sem_inc(s["sums_added"], 1)

            with dve.Fori(0, AGG_ITERS) as i:
                for r in range(RING):
                    lo = dve.value_load(ranges[0:1, bass.ds(i * RING + r, 1)], min_val=0, max_val=NT - 1)
                    hi = dve.value_load(ranges[0:1, bass.ds(i * RING + r + BROWS * P, 1)], min_val=0, max_val=NT - 1)
                    with dve.Fori(lo, hi + 1) as t:
                        make_onehot(i, r, t)
                        add_sums(r, t)
                    dve.sem_inc(s["sums_done"], 1)
            dve.drain()
            dve.tensor_scalar(deg[:, :], agg[:, :, C], 1.0, None, ALU.max)
            dve.drain()
            rsqrt(norm[:, :], deg[:, :], NT)
            dve.sem_inc(s["sums_final"], 1)
            dve.wait_ge(s["weights_in"], 80)

            with dve.Fori(0, SUPER) as i:
                dve.wait_ge(s["aggt_done"], i)
                for a in range(2):
                    q = dve.tensor_scalar(yrow[:, a, :], agg[:, bass.ds(2 * i + a, 1), 0:C].rearrange("p a b -> p (a b)"),
                                          norm[:, bass.ds(2 * i + a, 1)], None, ALU.mult)
                q.then_inc(s["agg_ready"], 1)
                dve.wait_ge(s["aggt_done"], i + 1)
                dve.tensor_copy(agg_t[:, :, :].rearrange("p k t -> p (k t)"), ps_t[:, :]).then_inc(s["aggt_copied"], 1)
                dve.wait_ge(s["xraw0_in"], 16 * i + 16)
                dve.wait_ge(s["xraw1_in"], 16 * i + 16)
                dve.wait_ge(s["gnn_done"], i + 1)
                for a in range(2):
                    dve.tensor_tensor(agg[:, bass.ds(2 * i + a, 1), 0:C].rearrange("p a b -> p (a b)"),
                                      ps_m[:, a * C:(a + 1) * C], xraw[:, a, :], ALU.add)
                dve.drain()
                dve.sem_inc(s["x1_done"], 1)
                for a in range(2):
                    dve.bn_stats(stats[:, a, :], agg[:, bass.ds(2 * i + a, 1), 0:C].rearrange("p a b -> p (a b)"))
                dve.drain()
                for a in range(2):
                    dve.bn_aggr(mv[:, a, :], stats[:, a, :])
                dve.drain()
                dve.tensor_scalar(deg[:, 0:2], mv[:, 0:2, 1], EPS, None, ALU.add)
                dve.drain()
                rsqrt(rstd[:, 0:2], deg[:, 0:2], 2)
                dve.wait_ge(s["scat_done"], 32 * i)
                for a in range(2):
                    q = dve.tensor_scalar(rows[:, a, :], agg[:, bass.ds(2 * i + a, 1), 0:C].rearrange("p a b -> p (a b)"),
                                          mv[:, a, 0:1], rstd[:, a:a + 1], ALU.subtract, ALU.mult)
                q.then_inc(s["rows_ready"], 1)
                dve.wait_ge(s["rowst_done"], i + 1)
                dve.tensor_copy(rows_t[:, :, :].rearrange("p k t -> p (k t)"), ps_t[:, :]).then_inc(s["rowst_copied"], 1)
                dve.wait_ge(s["gate_done"], i + 1)
                dve.tensor_scalar(logit_t[:, :], ps_gate[0:NE, 0:BT], bg_sb[:, 0:1], None, ALU.add
                                  ).then_inc(s["gate_copied"], 1)
                dve.wait_ge(s["gatet_done"], i + 1)
                dve.tensor_copy(logit[:, :, :].rearrange("p a e -> p (a e)"), ps_small[:, 0:2 * NE])
                dve.drain()
                for a in range(2):
                    dve.max(max8[:, a, :], logit[:, a, :])
                dve.drain()
                for a in range(2):
                    dve.max_index(arg8[:, a, :], max8[:, a, :], logit[:, a, :])
                    dve.tensor_scalar(below_max[:, bass.ds(2 * i + a, 1), :].rearrange("p a e -> p (a e)"),
                                      logit[:, a, :], max8[:, a, 0:1], None, ALU.subtract)
                dve.drain()
                dve.tensor_copy(argf[:, :], arg8[:, :, 0])
                dve.drain()
                for a in range(2):
                    q = dve.tensor_scalar(pick[:, a, :], iota8[:, :], argf[:, a:a + 1], None, ALU.is_equal)
                q.then_inc(s["pick_ready"], 1)
                dve.wait_ge(s["place_done"], i + 1)
                for a in range(2):
                    dve.tensor_tensor(place[:, a, :], ps_small[:, 64 + a * NE:64 + (a + 1) * NE], base[:, :], ALU.add)
                    dve.drain()
                    dve.tensor_tensor(base[:, :], ps_small[:, 128 + a * NE:128 + (a + 1) * NE], base[:, :], ALU.add)
                    dve.drain()
                dve.tensor_tensor(place[:, :, :], place[:, :, :], pick[:, :, :], ALU.mult)
                dve.drain()
                dve.tensor_reduce(posf[:, :], place[:, :, :], AX.X, ALU.add)
                dve.drain()
                dve.tensor_copy(pos_all[:, bass.ds(2 * i, 2)], posf[:, :])
                dve.tensor_copy(arg_all[:, bass.ds(2 * i, 2)], argf[:, :])
                dve.tensor_copy(pos_now[:, :], posf[:, :])
                dve.drain()
                dve.sem_inc(s["pos_ready"], 1)

            dve.tensor_scalar(cnt[:, :], iota8[:, :], -float(CAP), None, ALU.mult)
            dve.tensor_copy(zero_at[:, :], base[0:1, :])
            dve.drain()
            dve.tensor_tensor(cnt[:, :], cnt[:, :], base[:, :], ALU.add)
            dve.drain()
            dve.tensor_scalar(cnt[:, :], cnt[:, :], float(BT - 1), None, ALU.add)
            dve.drain()
            dve.tensor_copy(cnt_i[:, :], cnt[:, :])
            dve.drain()
            dve.tensor_scalar(cnt_i[:, :], cnt_i[:, :], BT.bit_length() - 1, None, ALU.arith_shift_right)
            dve.drain()
            dve.tensor_copy(cnt[:, :], cnt_i[:, :])
            dve.memset(cum[:, :], 0.0)
            dve.memset(q_e[:, :], 0.0)
            dve.memset(q_row[:, :], 0.0)
            dve.drain()
            for e in range(NE):
                dve.tensor_tensor(cum[:, e + 1:e + 2], cum[:, e:e + 1], cnt[:, e:e + 1], ALU.add)
                dve.drain()
            for e in range(NE + 1):
                dve.tensor_scalar(q_lo[:, :], q_iota[:, :], cum[0:1, e:e + 1], None, ALU.is_ge)
                if e < NE:
                    dve.tensor_scalar(q_hi[:, :], q_iota[:, :], cum[0:1, e + 1:e + 2], None, ALU.is_lt)
                    dve.drain()
                    dve.tensor_tensor(q_lo[:, :], q_lo[:, :], q_hi[:, :], ALU.mult)
                dve.drain()
                dve.tensor_scalar(q_hi[:, :], q_iota[:, :], cum[0:1, e:e + 1], float(BT), ALU.subtract, ALU.mult)
                dve.scalar_tensor_tensor(q_e[:, :], q_lo[:, :], float(min(e, NE - 1)), q_e[:, :], ALU.mult, ALU.add)
                dve.drain()
                dve.scalar_tensor_tensor(q_hi[:, :], q_hi[:, :], float(e * CAP), q_lo[:, :], ALU.add, ALU.mult)
                dve.drain()
                dve.tensor_tensor(q_row[:, :], q_row[:, :], q_hi[:, :], ALU.add)
                dve.drain()
            dve.tensor_copy(q_tab[:, 0, :], q_e[:, :])
            dve.tensor_copy(q_tab[:, 1, :], q_row[:, :])
            dve.tensor_scalar(cum[:, NE + 1:NE + 2], cum[:, NE:NE + 1], 1.0, None, ALU.add)
            dve.drain()
            dve.tensor_copy(q_n[:, :], cum[0:1, NE + 1:NE + 2])
            dve.drain()
            dve.tensor_scalar(q_n[:, :], q_n[:, :], 1, None, ALU.arith_shift_right)
            dve.drain()
            dve.sem_inc(s["plan_ready"], 1)
            dve.tensor_scalar(shift[:, :], iota8[:, :], -float(CAP), None, ALU.mult)
            dve.drain()
            dve.scalar_tensor_tensor(shift[:, :], cum[:, 0:NE], float(BT), shift[:, :], ALU.mult, ALU.add)
            dve.drain()
            for e in range(NE):
                dve.tensor_scalar(nr_a[:, :], arg_all[:, :], float(e), shift[:, e:e + 1], ALU.is_equal, ALU.mult)
                dve.drain()
                dve.tensor_tensor(pos_all[:, :], pos_all[:, :], nr_a[:, :], ALU.add)
                dve.drain()

            steps = dve.value_load(q_n[0:1, 0:1], min_val=1, max_val=QMAX // 2)
            with dve.Fori(0, steps) as i:
                for h in range(2):
                    dve.wait_ge(s["rowst_done"], SUPER + 2 * i + h + 1)
                    dve.tensor_copy(rows_t[:, :, :].rearrange("p k t -> p (k t)"), ps_t[:, :]
                                    ).then_inc(s["rowst_copied"], 1)
                    dve.wait_ge(s["y_done"], 2 * i + h + 1)
                    dve.wait_ge(s[f"wd_in{h}"], 32 * i + 32)
                    dve.wait_ge(s["y_stored"], 32 * i + 16 * h)
                    dve.tensor_tensor(yrow[:, 0, :], ps_m[:, 0:C], bd_sb[:, h, :], ALU.add)
                    dve.tensor_tensor(yrow[:, 1, :], ps_m[:, C:2 * C], bd_sb[:, h, :], ALU.add)
                    dve.drain()
                    dve.sem_inc(s["y_ready"], 1)

            dve.wait_ge(s["exp_done"], 1)
            dve.tensor_reduce(prob[:, :], below_max[:, :, :], AX.X, ALU.add)
            dve.drain()
            dve.reciprocal(prob[:, :], prob[:, :])
            dve.drain()

            def put_places(i, h):
                if not isinstance(i, int) or i:
                    for u in range(G5):
                        dve.wait_ge(y_in[h * G5 + u], 16 * i)
                    dve.wait_ge(s[f"out_done{h}"], 16 * i)
                dve.tensor_copy(pos_ring[:, h * G5:(h + 1) * G5], pos_all[:, bass.ds((2 * i + h) * G5, G5)]
                                ).then_inc(s["pos_put"], 1)

            with dve.Fori(0, N5) as i:
                for h in range(2):
                    put_places(i, h)
                for h in range(2):
                    for u in range(G5):
                        k = h * G5 + u
                        t = (2 * i + h) * G5 + u
                        dve.wait_ge(y_in[k], 16 * i + 16)
                        dve.scalar_tensor_tensor(gath[:, k, 0:C], gath[:, k, 0:C], prob[:, bass.ds(t, 1)],
                                                 agg[:, bass.ds(t, 1), 0:C].rearrange("p a b -> p (a b)"),
                                                 ALU.mult, ALU.add)
                    dve.drain()
                    dve.sem_inc(s["out_ready"], 1)

        @block.tensor
        def _(pe):
            pe.wait_ge(s["consts_ready"], 7)
            pe.wait_ge(s["edges_float"], 2)
            df = dst_f.rearrange("p (j q) -> p j q", q=P)
            sf = src_f.rearrange("p (j q) -> p j q", q=P)
            for j in range(0, CROWS, 4):
                g = j // 4
                if g >= 2:
                    pe.wait_ge(s["dst_copied"], g - 1)
                    pe.wait_ge(s["src_copied"], g - 1)
                for f, bank in ((df, ps_t if g % 2 == 0 else ps_h[0]), (sf, ps_m if g % 2 == 0 else ps_h[1])):
                    for k in range(j, min(j + 4, CROWS)):
                        m = min(P, NCH - k * P)
                        q = pe.transpose(bank[:, (k - j) * P:(k - j) * P + m], f[0:m, k, :], ident[0:m, 0:m])
                    q.then_inc(s["tr_done"], 1)
            pe.wait_ge(s["blk_ready"], 1)
            pe.transpose(ps_agg[0][0:2 * BROWS, 0:P], blk_f, ident[:, :]).then_inc(s["blk_tr"], 1)

            pe.wait_ge(s["range_in"], 16)
            total = pe.alloc_register("visits")
            pe.reg_mov(total, 0)
            with pe.Fori(0, AGG_ITERS) as i:
                for r in range(RING):
                    lo = pe.value_load(ranges[0:1, bass.ds(i * RING + r, 1)], min_val=0, max_val=NT - 1)
                    hi = pe.value_load(ranges[0:1, bass.ds(i * RING + r + BROWS * P, 1)], min_val=0, max_val=NT - 1)
                    pe.wait_ge(gathered[r], i * (16 * U) + 16 * U)
                    pe.sem_inc(s["t_turn"], 1)
                    with pe.Fori(lo, hi + 1) as t:
                        done = pe.snap(total)
                        pe.wait_ge(s["onehot_ready"], done + 1)
                        for u in range(U):
                            k = r * U + u
                            q = pe.matmul(ps_agg[r][:, 0:AW], onehot[:, k, :], gath[:, k, 0:AW],
                                          start=(u == 0), stop=(u == U - 1))
                        q.then_inc(visit_done[r], 1)
                        pe.reg_add(total, total, 1)

            pe.wait_ge(s["weights_in"], 80)
            pe.wait_ge(s["sums_final"], 1)

            def hidden(first):
                for k in range(KH):
                    pe.wait_ge(s["gelu_done"], first + k - 1)
                    for c in range(KC):
                        q = pe.matmul(ps_h[k % 2][:, 0:BT], w1_sb[:, c, k * P:(k + 1) * P], rows_t[:, c, :],
                                      start=(c == 0), stop=(c == KC - 1))
                    q.then_inc(s["hid_done"], 1)

            def transpose_rows(get):
                for c in range(KC):
                    for a in range(2):
                        q = pe.transpose(ps_t[:, c * BT + a * P:c * BT + (a + 1) * P], get(a, c), ident[:, :])
                return q

            pe.sem_inc(s["gelu_done"], 0) if False else None
            with pe.Fori(0, SUPER) as i:
                pe.wait_ge(s["rowst_copied"], i)
                pe.wait_ge(s["agg_ready"], i + 1)
                transpose_rows(lambda a, c: yrow[:, a, c * P:(c + 1) * P]).then_inc(s["aggt_done"], 1)
                pe.wait_ge(s["aggt_copied"], i + 1)
                pe.wait_ge(s["x1_done"], i)
                for a in range(2):
                    for c in range(KC):
                        q = pe.matmul(ps_m[:, a * C:(a + 1) * C], agg_t[:, c, a * P:(a + 1) * P], w_sb[:, c, :],
                                      start=(c == 0), stop=(c == KC - 1))
                q.then_inc(s["gnn_done"], 1)
                pe.wait_ge(s["rows_ready"], i + 1)
                transpose_rows(lambda a, c: rows[:, a, c * P:(c + 1) * P]).then_inc(s["rowst_done"], 1)
                pe.wait_ge(s["rowst_copied"], i + 1)
                hidden_at = KH * i
                for k in range(KH):
                    if k >= 2:
                        pe.wait_ge(s["gelu_done"], hidden_at + k - 1)
                    for c in range(KC):
                        q = pe.matmul(ps_h[k % 2][:, 0:BT], w1_sb[:, c, k * P:(k + 1) * P], rows_t[:, c, :],
                                      start=(c == 0), stop=(c == KC - 1))
                    q.then_inc(s["hid_done"], 1)
                pe.wait_ge(s["gelu_done"], hidden_at + KH)
                for k in range(KH):
                    q = pe.matmul(ps_gate[0:NE, 0:BT], wg_sb[:, k, :], hid[:, k, :], start=(k == 0), stop=(k == KH - 1))
                q.then_inc(s["gate_done"], 1)
                pe.wait_ge(s["gate_copied"], i + 1)
                pe.sem_inc(s["t_turn"], 1)
                for a in range(2):
                    q = pe.transpose(ps_small[:, a * NE:(a + 1) * NE], logit_t[:, a * P:(a + 1) * P], ident[0:NE, 0:NE])
                q.then_inc(s["gatet_done"], 1)
                pe.wait_ge(s["pick_ready"], i + 1)
                both = pick[:, :, :].rearrange("p a e -> p (a e)")
                pe.matmul(ps_small[:, 64:64 + 2 * NE], before[:, :], both, start=True, stop=True)
                pe.matmul(ps_small[:, 128:128 + 2 * NE], ones[:, :], both, start=True, stop=True
                          ).then_inc(s["place_done"], 1)

            pe.wait_ge(s["plan_ready"], 1)
            steps = pe.value_load(q_n[0:1, 0:1], min_val=1, max_val=QMAX // 2)
            with pe.Fori(0, steps) as i:
                for h in range(2):
                    b = 2 * i + h
                    pe.wait_ge(s["blk_in"], 16 * b + 16)
                    pe.wait_ge(s["rowst_copied"], b + SUPER)
                    transpose_rows(lambda a, c: rows[:, a, c * P:(c + 1) * P]).then_inc(s["rowst_done"], 1)
                    pe.wait_ge(s["rowst_copied"], b + SUPER + 1)
                    for k in range(KH):
                        if k >= 2:
                            pe.wait_ge(s["gelu_done"], KH * b + KH * SUPER + k - 1)
                        for c in range(KC):
                            q = pe.matmul(ps_h[k % 2][:, 0:BT], w1_sb[:, c, k * P:(k + 1) * P], rows_t[:, c, :],
                                          start=(c == 0), stop=(c == KC - 1))
                        q.then_inc(s["hid_done"], 1)
                    pe.wait_ge(s["gelu_done"], KH * b + KH * SUPER + KH)
                    pe.wait_ge(s[f"wd_in{h}"], 32 * i + 32)
                    pe.wait_ge(s["y_ready"], b)
                    for a in range(2):
                        for k in range(KH):
                            q = pe.matmul(ps_m[:, a * C:(a + 1) * C], hid[:, k, a * P:(a + 1) * P],
                                          wd_sb[:, h, k, :], start=(k == 0), stop=(k == KH - 1))
                    q.then_inc(s["y_done"], 1)


def kernel(x, src, dst, L0_gnn_weight, L0_ffn_W1, L0_ffn_b1, L0_ffn_Wg, L0_ffn_bg, L0_ffn_Wd, L0_ffn_bd):
    import numpy as np
    import concourse.bacc as bacc
    from concourse.bass_utils import run_bass_kernel_spmd

    nc = bacc.Bacc("TRN2", target_bir_lowering=False, num_devices=1)
    arrays, args = {}, []
    for name, a in (("x", x), ("src", src), ("dst", dst), ("w_gnn", L0_gnn_weight), ("w1", L0_ffn_W1),
                    ("b1", L0_ffn_b1), ("wg", L0_ffn_Wg), ("bg", L0_ffn_bg), ("wd", L0_ffn_Wd), ("bd", L0_ffn_bd)):
        a = np.ascontiguousarray(a)
        arrays[name] = a
        args.append(nc.dram_tensor(name, a.shape, mybir.dt.from_np(a.dtype), kind="ExternalInput").ap())
    out = nc.dram_tensor("out", x.shape, mybir.dt.float32, kind="ExternalOutput").ap()
    gnn_moe_program(nc, *args, out)
    r = run_bass_kernel_spmd(nc, [arrays], core_ids=[0])
    return r.results[0]["out"]
```

```python
import concourse.bass as bass
from concourse import mybir
from contextlib import ExitStack, nullcontext


def gnn_moe_program(nc, x, src, dst, w_gnn, w1, b1, wg, bg, wd, bd, out):
    F32, F32R, I32, U32 = mybir.dt.float32, mybir.dt.float32r, mybir.dt.int32, mybir.dt.uint32
    ALU = mybir.AluOpType
    ACT = mybir.ActivationFunctionType
    AX = mybir.AxisListType

    P = 128
    N, C = x.shape
    E = src.shape[0]
    HID = w1.shape[1]
    NE = wg.shape[1]
    EPS = 1e-5
    KC = C // P
    KH = HID // P
    NT = -(-N // P)
    LAST = N - (NT - 1) * P
    NPAD = NT * P
    LN_GROUPS = 7
    LT = NT // LN_GROUPS
    assert NT % LN_GROUPS == 0 and NT % 2 == 0
    U = 4
    RING = 4
    S = 2 * RING
    ITERS = -(-E // (U * P * S))
    NB = ITERS * S
    NCH = NB * U
    CROWS = -(-NCH // P)
    BROWS = -(-NB // P)
    PAD_DST = -1
    AW = C + 2
    BT = 2 * P
    PAIRS = NT // 2
    CAP = NPAD + BT
    RW = 2 * C + 4
    ID, PROB = 2 * C, 2 * C + 1
    NO_TOKEN = float(1 << 20)
    END = 2
    PLANS = ITERS + PAIRS + END
    PW = 3
    QMAX = PAIRS + NE + 1
    QMAX += QMAX % 2

    ctx = ExitStack()
    with ctx:
        def sb(name, shape, dt=F32):
            return ctx.enter_context(nc.sbuf_tensor(name, shape, dt))

        def pb(name):
            return ctx.enter_context(nc.psum_tensor(name, [P, 512], F32))

        table = nc.dram_tensor("xn_table", (NPAD, C), F32).ap()
        ranges_d = nc.dram_tensor("tile_ranges", (2 * BROWS, P), I32).ap()
        routed = nc.dram_tensor("routed_rows", (NE * CAP + BT, RW), F32).ap()

        agg = sb("agg", [P, NT, C + 1])
        dst_t = sb("dst_t", [P, NCH + RING * U])
        src_t = sb("src_t", [P, NCH + 2 * RING * U], I32)
        gath = sb("gath", [P, RING * U, C])
        high = sb("high", [P, 2, U, AW], F32R)
        low = sb("low", [P, 2, U, C], F32R)
        onehot = sb("onehot", [P, 2, U, P], F32R)
        idx_ring = sb("idx_ring", [P, RING * U], U32)
        ranges = sb("ranges", [2, BROWS * P], I32)
        iota = sb("iota", [P, P])
        ident = sb("ident", [P, P])
        before = sb("before", [P, P])
        ones = sb("ones", [P, P])
        tile_base = sb("tile_base", [P, NT])
        iota8 = sb("iota8", [P, NE])
        node = sb("node", [P, 2])
        w_sb = sb("w_sb", [P, KC, C])
        w1_sb = sb("w1_sb", [P, KC, HID])
        b1_sb = sb("b1_sb", [P, KH])
        wg_sb = sb("wg_sb", [P, KH, NE])
        bg_sb = sb("bg_sb", [NE, 1])
        wd_sb = sb("wd_sb", [P, KH, C])
        bd_sb = sb("bd_sb", [P, C])
        hid = sb("hid", [P, KH, BT])
        block_t = sb("block_t", [P, KC, BT])
        scaled = sb("scaled", [P, 2, C])
        pair_t = sb("pair_t", [P, KC, BT])
        shift = sb("shift", [P, 2])
        xraw = sb("xraw", [P, 2, C])
        xn2 = sb("xn2", [P, 2, C])
        token_rows = sb("token_rows", [P, 2, RW])
        block_rows = sb("block_rows", [P, 2, RW])
        result = sb("result", [P, 2, C])
        out_at = sb("out_at", [P, 2], U32)
        stats = sb("stats", [P, LT, 6])
        mv = sb("mv", [P, LT, 2])
        rstd = sb("rstd", [P, LT])
        var = sb("var", [P, LT])
        deg = sb("deg", [P, 2])
        norm = sb("norm", [P, 2])
        nr_a = sb("nr_a", [P, LT])
        nr_b = sb("nr_b", [P, LT])
        nr_i = sb("nr_i", [P, LT], I32)
        logit_t = sb("logit_t", [NE, BT])
        logit = sb("logit", [P, 2, NE])
        max8 = sb("max8", [P, 2, 8])
        arg8 = sb("arg8", [P, 2, 8], U32)
        argf = sb("argf", [P, 2])
        pick = sb("pick", [P, 2, NE])
        place = sb("place", [P, 2, NE])
        below = sb("below", [P, 2, NE])
        tanhs = sb("tanhs", [P, 2, NE])
        expo = sb("expo", [P, 2, NE])
        base = sb("base", [P, NE])
        posf = sb("posf", [P, 2])
        total = sb("total", [P, 2])
        pos_now = sb("pos_now", [P, 2], U32)
        nxt = sb("nxt", [1, NE])
        avail = sb("avail", [1, NE])
        best = sb("best", [1, 8])
        best_at = sb("best_at", [1, 8], U32)
        chosen = sb("chosen", [1, NE])
        plan_f = sb("plan_f", [1, 4])
        plan = sb("plan", [1, PW * PLANS], I32)
        start = sb("start", [1, ITERS], I32)
        pairs_left = sb("pairs_left", [1, 1], I32)
        cnt = sb("cnt", [1, NE])
        cnt_i = sb("cnt_i", [1, NE], I32)
        cum = sb("cum", [1, NE + 2])
        zero_at = sb("zero_at", [1, NE], I32)
        q_iota = sb("q_iota", [1, QMAX])
        q_tab = sb("q_tab", [1, 2, QMAX], I32)
        q_n = sb("q_n", [1, 1], I32)

        flat = lambda t, s: t.rearrange(s)
        spare = flat(gath[:, :, :], "p a b -> p (a b)")
        dst_i = spare[:, 0:CROWS * P].bitcast(I32)
        src_i = spare[:, CROWS * P:2 * CROWS * P].bitcast(I32)
        blk_i = flat(hid[:, :, :], "p a b -> p (a b)").bitcast(I32)
        dst_f = flat(wd_sb[:, :, :], "p a b -> p (a b)")[:, 0:CROWS * P]
        src_f = [t[:, :, :].rearrange("p a b -> p (a b)").rearrange("p (j q) -> p j q", q=P)
                 for t in (block_t, pair_t, scaled, result)]
        assert CROWS <= 4 * len(src_f)
        line = flat(block_rows[0:1, :, :], "p a b -> p (a b)")
        f_a, f_b = line[:, 0:ITERS + P], line[:, ITERS + P:2 * (ITERS + P)]
        f_i = line[:, 2 * (ITERS + P):3 * ITERS + 2 * P].bitcast(I32)
        begun = line[:, 3 * ITERS + 2 * P:4 * ITERS + 2 * P + 1]
        line = flat(scaled[0:1, :, :], "p a b -> p (a b)")
        q_e, q_row, q_lo, q_hi = (line[:, k * QMAX:(k + 1) * QMAX] for k in range(4))
        blk_r = nr_i[:, 0:2 * BROWS]
        blk_f = nr_a[:, 0:2 * BROWS]
        range_f = xn2[0:2 * BROWS, 0, 0:P]
        range_i = xn2[0:2 * BROWS, 1, 0:P].bitcast(I32)
        wd_2 = spare[:, 0:KH * C].rearrange("p (k c) -> p k c", k=KH)
        block_rows_2 = spare[:, KH * C:KH * C + 2 * RW].rearrange("p (a c) -> p a c", a=2)
        bd_2 = spare[:, KH * C + 2 * RW:(KH + 1) * C + 2 * RW]
        assert 2 * BROWS <= LT and (KH + 1) * C + 2 * RW <= RING * U * C
        assert 4 * ITERS + 2 * P + 1 <= 2 * RW and 4 * QMAX <= 2 * C

        ps_sum = [pb(f"ps_sum{i}") for i in range(2)]
        ps_t = pb("ps_t")
        ps_w = pb("ps_w")
        ps_m = pb("ps_m")
        ps_h = [pb(f"ps_h{i}") for i in range(2)]
        ps_g = pb("ps_g")

        names = """pads_set edges_in weights_in const_base consts_ready dst_float src_float tr_done dst_copied src_copied
        blk_float blk_tr blk_rows range_out range_in tables_ready normed table_written spare_out
        idx_ready turn sp_turn pe_turn dve_turn act_turn
        high_ready split_done block_done first_ready more_ready visit_done
        x_again scaled_ready scaledt_done scaledt_copied gnn_done x1_done xn2_ready pairt_done pairt_copied
        hid_done gelu_done hid_free gate_done gate_copied gatet_done rstd_ready sums_final pick_ready below_ready tanh_ready
        rows_copied place_done place_used pos_ready scattered rows_free plan_ready
        block_in blockt_done blockt_copied y_done y_read result_ready result_out result_free
        last_plan tails_zero last_out last_in0 last_in1 last_t last_tc last_hid last_gelu last_y last_read
        last_result last_free""".split()
        s = {n: ctx.enter_context(nc.semaphore(n)) for n in names}
        x_in = [ctx.enter_context(nc.semaphore(f"x_in{g}")) for g in range(LN_GROUPS)]
        gathered = [ctx.enter_context(nc.semaphore(f"gathered{r}")) for r in range(RING)]

        block = ctx.enter_context(nc.Block())

        def load_edges(eng, a, buf, w):
            full = E // (P * w)
            parts = [(slice(0, P), slice(0, full), a[0:full * P * w].rearrange("(j p q) -> p j q", p=P, q=w))]
            rest = E - full * P * w
            n = rest // w
            if n:
                parts.append((slice(0, n), full, a[full * P * w:full * P * w + n * w].rearrange("(p q) -> p q", q=w)))
            if rest % w:
                parts.append((slice(n, n + 1), full, a[E - rest % w:E].rearrange("(p q) -> p q", p=1)))
            if eng is not None:
                for p, j, part in parts:
                    eng.dma_start(buf[p, j, 0:part.shape[-1]], part).then_inc(s["edges_in"], 16)
            return len(parts)

        class Progress:

            def __init__(self, eng, late=False):
                self.eng, self.late = eng, late
                self.reg = {n: eng.alloc_register(n) for n in ("pairs", "gated", "blocks", "results", "g", "g_next", "h")}
                for r in self.reg.values():
                    eng.reg_mov(r, 0)

            def get(self, name, top=1 << 24):
                return self.eng.snap(self.reg[name], min_val=0, max_val=top)

            def advance(self, f, b):
                R, eng = self.reg, self.eng
                eng.reg_add(R["gated"], R["gated"], R["g"])
                eng.reg_add(R["results"], R["results"], R["h"])
                if self.late:
                    eng.reg_mov(R["g"], R["g_next"])
                    eng.reg_mov(R["g_next"], f)
                else:
                    eng.reg_mov(R["g"], f)
                eng.reg_mov(R["h"], b)
                eng.reg_add(R["pairs"], R["pairs"], f)
                eng.reg_add(R["blocks"], R["blocks"], b)

        def has(eng, flag):
            return nullcontext() if isinstance(flag, int) else eng.If(flag > 0)

        def may(flag):
            return not (isinstance(flag, int) and flag == 0)

        def block_flag(eng, i):
            eng.wait_ge(s["plan_ready"], i + 1)
            eng.sem_inc(turn_of(eng), 1)
            return eng.value_load(plan[0:1, bass.ds(PW * i, 1)], min_val=0, max_val=1)

        turns = {}

        def turn_of(eng):
            return turns[id(eng)]

        class Ranges:

            def __init__(self, eng):
                self.eng = eng
                self.hi = [eng.alloc_register(f"hi{r}") for r in range(S)]
                self.lo = [eng.alloc_register(f"lo{r}") for r in range(S + 1)]

            def load(self, i):
                self.eng.load(self.hi, ranges[0:1, bass.ds(i * S, S)])
                self.eng.load(self.lo, ranges[1:2, bass.ds(i * S, S + 1)])

            def first(self, r):
                return self.eng.snap(self.lo[r], min_val=0, max_val=NT - 1)

            def last(self, r):
                return self.eng.snap(self.hi[r], min_val=0, max_val=NT - 1)

        def iterations(eng, one, end_iters):
            with eng.Fori(0, ITERS) as i:
                one(i, eng.value_load(start[0:1, bass.ds(i, 1)], min_val=0, max_val=1), True)
            left = eng.value_load(pairs_left[0:1, 0:1], min_val=1, max_val=PAIRS)
            with eng.Fori(0, left) as k:
                one(k + ITERS, 1, False)
            for n in range(end_iters):
                one(eng.snap(left + (ITERS + n)), 0, False, n < END - 1)

        @block.sync
        def _(sp):
            turns[id(sp)] = s["sp_turn"]
            sp.sem_inc(s["rows_free"], 1)
            sp.sem_inc(s["result_free"], 1)
            sp.wait_ge(s["pads_set"], 1)
            for g in range(LN_GROUPS):
                t0, t1 = g * LT, (g + 1) * LT
                full = t1 if t1 < NT else NT - 1
                sp.dma_start(agg[:, t0:full, 0:C],
                             x[t0 * P:full * P, :].rearrange("(t p) c -> p t c", p=P)).then_inc(x_in[g], 16)
                if full < t1:
                    sp.dma_start(agg[0:LAST, NT - 1, 0:C], x[(NT - 1) * P:N, :]).then_inc(x_in[g], 16)
                if g == 0:
                    load_edges(sp, dst, dst_i.rearrange("p (j q) -> p j q", q=P), P)
                    load_edges(sp, src, src_i.rearrange("p (j q) -> p j q", q=P), P)
                    load_edges(sp, dst, blk_i.rearrange("p (j q) -> p j q", q=U * P), U * P)
            sp.wait_ge(s["blk_rows"], 1)
            sp.dma_start(ranges_d, range_i).then_inc(s["range_out"], 16)
            sp.wait_ge(s["range_out"], 16)
            sp.dma_start(ranges[:, :], ranges_d.rearrange("(k b) q -> k (b q)", k=2)).then_inc(s["range_in"], 16)
            for g in range(LN_GROUPS):
                sp.wait_ge(s["normed"], 1 + g)
                sp.dma_start(table[g * LT * P:(g + 1) * LT * P, :].rearrange("(t p) c -> p t c", p=P),
                             agg[:, g * LT:(g + 1) * LT, 0:C]).then_inc(s["table_written"], 16)
            sp.dma_start(w_sb[:, :, :], w_gnn.rearrange("(k p) c -> p k c", p=P)).then_inc(s["weights_in"], 16)
            sp.dma_start(w1_sb[:, :, :], w1.rearrange("(k p) c -> p k c", p=P)).then_inc(s["weights_in"], 16)
            sp.dma_start(wg_sb[:, :, :], wg.rearrange("(k p) c -> p k c", p=P)).then_inc(s["weights_in"], 16)
            with nc.allow_non_contiguous_dma(reason="a few bias values"):
                sp.dma_start(b1_sb[:, :], b1.rearrange("(k p) -> p k", p=P)).then_inc(s["weights_in"], 16)
                sp.dma_start(bg_sb[:, :], bg.rearrange("(p q) -> p q", q=1)).then_inc(s["weights_in"], 16)
            sp.wait_ge(s["tables_ready"], 1)

            pr = Progress(sp, late=True)

            def one(i, f, edges, planned=True):
                pairs, gated, blocks = pr.get("pairs", PAIRS - 1), pr.get("gated"), pr.get("blocks")
                g, h = pr.get("g", 1), pr.get("h", 1)
                if may(f):
                    with has(sp, f):
                        sp.wait_ge(s["x1_done"], pairs + 1)
                        sp.sem_inc(s["sp_turn"], 1)
                        at = (PAIRS - 1) * BT - pairs * BT
                        sp.dma_start(xraw[:, 0, :], x[bass.ds(at, P), :]).then_inc(s["x_again"], 16)
                        with sp.If(pairs < 1):
                            sp.dma_start(xraw[0:LAST, 1, :], x[(NT - 1) * P:N, :]).then_inc(s["x_again"], 16)
                        with sp.If(pairs > 0):
                            beside = (PAIRS - 1) * BT + P - sp.snap(pr.reg["pairs"], min_val=1, max_val=PAIRS - 1) * BT
                            sp.dma_start(xraw[:, 1, :], x[bass.ds(beside, P), :]).then_inc(s["x_again"], 16)
                with sp.If(g > 0):
                    sp.wait_ge(s["scattered"], 32 * gated + 32)
                    sp.sem_inc(s["rows_free"], 1)
                b = block_flag(sp, i) if planned else 0
                if may(b):
                    e = sp.value_load(plan[0:1, bass.ds(PW * i + 1, 1)], min_val=0, max_val=NE - 1)
                    row = sp.value_load(plan[0:1, bass.ds(PW * i + 2, 1)], min_val=0, max_val=NE * CAP)
                    with sp.If(b > 0):
                        sp.wait_ge(s["y_read"], blocks + 1)
                        sp.sem_inc(s["sp_turn"], 1)
                        sp.dma_start(block_rows[:, :, :], routed[bass.ds(row, BT), :].rearrange("(p k) c -> p k c", p=P)
                                     ).then_inc(s["block_in"], 16)
                        sp.dma_start(wd_sb[:, :, :], wd[bass.ds(e, 1), :, :].rearrange("o (k p) c -> p (o k) c", p=P)
                                     ).then_inc(s["block_in"], 16)
                        sp.dma_start(bd_sb[:, :], bd[bass.ds(e, 1), :].to_broadcast([P, C])).then_inc(s["block_in"], 16)
                with sp.If(h > 0):
                    sp.wait_ge(s["result_out"], 32 * pr.get("results") + 32)
                    sp.sem_inc(s["result_free"], 1)
                pr.advance(f, b)

            iterations(sp, one, END)

            sp.wait_ge(s["last_plan"], 1)
            for e in range(NE):
                at = sp.value_load(zero_at[0:1, e:e + 1], min_val=0, max_val=NE * CAP)
                sp.dma_start(routed[bass.ds(at, BT), :].rearrange("(p k) c -> p k c", p=P),
                             token_rows[:, :, :]).then_inc(s["tails_zero"], 16)
            sp.dma_start(routed[NE * CAP:NE * CAP + BT, :].rearrange("(p k) c -> p k c", p=P),
                         token_rows[:, :, :]).then_inc(s["tails_zero"], 16)
            sp.wait_ge(s["tails_zero"], 16 * (NE + 1))
            steps = sp.value_load(q_n[0:1, 0:1], min_val=1, max_val=QMAX // 2)
            with sp.Fori(0, steps) as i:
                for h in range(2):
                    e = sp.value_load(q_tab[0:1, 0, bass.ds(2 * i + h, 1)], min_val=0, max_val=NE - 1)
                    row = sp.value_load(q_tab[0:1, 1, bass.ds(2 * i + h, 1)], min_val=0, max_val=NE * CAP)
                    sp.wait_ge(s["last_read"], 2 * i + h + 1)
                    sp.sem_inc(s["sp_turn"], 1)
                    sp.dma_start((block_rows[:, :, :], block_rows_2)[h],
                                 routed[bass.ds(row, BT), :].rearrange("(p k) c -> p k c", p=P)
                                 ).then_inc(s[f"last_in{h}"], 16)
                    sp.dma_start((wd_sb[:, :, :], wd_2)[h],
                                 wd[bass.ds(e, 1), :, :].rearrange("o (k p) c -> p (o k) c", p=P)
                                 ).then_inc(s[f"last_in{h}"], 16)
                    sp.dma_start((bd_sb[:, :], bd_2)[h], bd[bass.ds(e, 1), :].to_broadcast([P, C])
                                 ).then_inc(s[f"last_in{h}"], 16)

        @block.gpsimd
        def _(pool):
            turns[id(pool)] = s["turn"]
            pool.memset(ident[:, :], 0.0).then_inc(s["const_base"], 1)
            pool.memset(before[:, :], 1.0).then_inc(s["const_base"], 1)
            for t, step in ((iota, 1), (tile_base, P), (iota8, 1), (base, CAP), (nxt, CAP), (q_iota, 1)):
                pool.iota(t[:, :], pattern=[[step, t.shape[1]]], base=0, channel_multiplier=0,
                          allow_small_or_imprecise_dtypes=True).then_inc(s["consts_ready"], 1)
            pool.iota(node[:, :], pattern=[[P, 2]], base=(PAIRS - 1) * BT, channel_multiplier=1,
                      allow_small_or_imprecise_dtypes=True).then_inc(s["consts_ready"], 1)
            pool.wait_ge(s["const_base"], 2)
            pool.affine_select(out=ident[:, :], in_=ident[:, :], compare_op=ALU.not_equal, fill=1.0, base=0,
                               pattern=[[-1, P]], channel_multiplier=1).then_inc(s["consts_ready"], 1)
            pool.affine_select(out=before[:, :], in_=before[:, :], compare_op=ALU.is_gt, fill=0.0, base=0,
                               pattern=[[1, P]], channel_multiplier=-1).then_inc(s["consts_ready"], 1)
            pool.wait_ge(s["tables_ready"], 1)
            pool.wait_ge(s["table_written"], 16 * LN_GROUPS)
            pr = Progress(pool, late=True)

            def one(i, f, edges, planned=True):
                gated, results = pr.get("gated"), pr.get("results")
                g, h = pr.get("g", 1), pr.get("h", 1)
                for r in range(S):
                    if edges:
                        pool.wait_ge(s["split_done"], S * i + r + 1)
                        pool.wait_ge(s["idx_ready"], S * i + r + 1)
                        pool.sem_inc(s["turn"], 1)
                        for u in range(U):
                            k = (r % RING) * U + u
                            pool.indirect_dma_start(
                                gath[:, k, :], None, table,
                                bass.IndirectOffsetOnAxis(ap=idx_ring[:, k:k + 1], axis=0)).then_inc(gathered[r % RING], 16)
                    if r == 1:
                        with pool.If(g > 0):
                            pool.wait_ge(s["pos_ready"], gated + 1)
                            pool.sem_inc(s["turn"], 1)
                            for a in range(2):
                                pool.indirect_dma_start(
                                    routed, bass.IndirectOffsetOnAxis(ap=pos_now[:, a:a + 1], axis=0),
                                    token_rows[:, a, :], None).then_inc(s["scattered"], 16)
                    if r == 2:
                        with pool.If(h > 0):
                            pool.wait_ge(s["result_ready"], results + 1)
                            pool.sem_inc(s["turn"], 1)
                            for a in range(2):
                                pool.indirect_dma_start(
                                    out, bass.IndirectOffsetOnAxis(ap=out_at[:, a:a + 1], axis=0),
                                    result[:, a, :], None, bounds_check=N - 1, oob_is_err=False).then_inc(s["result_out"], 16)
                b = block_flag(pool, i) if planned else 0
                pr.advance(f, b)

            iterations(pool, one, END)
            pool.sem_inc(s["last_free"], 1)
            pool.wait_ge(s["last_plan"], 1)
            steps = pool.value_load(q_n[0:1, 0:1], min_val=1, max_val=QMAX // 2)
            with pool.Fori(0, steps) as i:
                for h in range(2):
                    pool.wait_ge(s["last_result"], 2 * i + h + 1)
                    pool.sem_inc(s["turn"], 1)
                    for a in range(2):
                        pool.indirect_dma_start(
                            out, bass.IndirectOffsetOnAxis(ap=out_at[:, a:a + 1], axis=0),
                            result[:, a, :], None, bounds_check=N - 1, oob_is_err=False).then_inc(s["last_out"], 16)
                    pool.wait_ge(s["last_out"], 64 * i + 32 * h + 32)
                    pool.sem_inc(s["last_free"], 1)

        @block.scalar
        def _(act):
            turns[id(act)] = s["act_turn"]
            act.preload_act_table(ACT.Gelu)
            for j in range(0, CROWS, 4):
                m = min(4 * P, NCH - j * P)
                g = j // 4
                act.wait_ge(s["tr_done"], 2 * g + 2)
                act.copy(src_t[:, j * P:j * P + m], (ps_m, ps_h[1])[g % 2][:, 0:m]).then_inc(s["src_copied"], 1)
            act.wait_ge(s["tables_ready"], 1)
            act.drain()
            pr = Progress(act)

            def put_indices(it, r):
                k = (r % RING) * U
                act.copy(idx_ring[:, k:k + U], src_t[:, bass.ds(it * (S * U) + r * U, U)]).then_inc(s["idx_ready"], 1)

            def take_high(it, r):
                k = (r % RING) * U
                act.wait_ge(gathered[r % RING], it * (16 * U * S // RING) + (r // RING + 1) * (16 * U))
                act.wait_ge(s["block_done"], S * it + r + 1)
                act.copy(high[:, r % 2, :, 0:C], gath[:, k:k + U, :]).then_inc(s["high_ready"], 1)
                put_indices(it, r + RING)

            def hidden(index, part):
                if part == 0:
                    act.wait_ge(s["hid_free"], index + 1)
                for k in range(part * KH // 2, (part + 1) * KH // 2):
                    act.wait_ge(s["hid_done"], KH * index + k + 1)
                    act.activation(hid[:, k, :], ps_h[k % 2][:, 0:BT], ACT.Gelu,
                                   bias=b1_sb[:, k:k + 1]).then_inc(s["gelu_done"], 1)

            for r in range(RING):
                put_indices(0, r)
            take_high(0, 0)
            act.wait_ge(s["weights_in"], 80)

            def one(i, f, edges, planned=True):
                pairs, gated, blocks = pr.get("pairs", PAIRS - 1), pr.get("gated", PAIRS - 1), pr.get("blocks")
                g = pr.get("g", 1)
                b = block_flag(act, i) if planned else 0
                for r in range(S):
                    if edges and r < S - 1:
                        take_high(i, r + 1)
                    elif edges:
                        with act.If(i < ITERS - 1):
                            take_high(i + 1, 0)
                    if r == 0 and may(f):
                        with has(act, f):
                            act.wait_ge(s["sums_final"], i + 1)
                            act.copy(scaled[:, :, :], agg[:, bass.ds(2 * (PAIRS - 1) - 2 * pairs, 2), 0:C]
                                     ).then_inc(s["scaled_ready"], 1)
                    if r == 1:
                        if may(f):
                            with has(act, f):
                                act.wait_ge(s["scaledt_done"], pairs + 1)
                                act.copy(flat(pair_t[:, :, :], "p k t -> p (k t)"), ps_t[:, :]
                                         ).then_inc(s["scaledt_copied"], 1)
                        if may(b):
                            with act.If(b > 0):
                                act.wait_ge(s["blockt_done"], blocks + 1)
                                act.copy(flat(block_t[:, :, :], "p k t -> p (k t)"), ps_h[0][:, :]
                                         ).then_inc(s["blockt_copied"], 1)
                    if r == 2:
                        with act.If(g > 0):
                            act.wait_ge(s["rows_free"], gated + 1)
                            act.copy(token_rows[:, :, C:2 * C], agg[:, bass.ds(2 * (PAIRS - 1) - 2 * gated, 2), 0:C])
                            act.copy(token_rows[:, :, 0:C], xn2[:, :, :])
                    if r == 3:
                        with act.If(g > 0):
                            act.wait_ge(s["below_ready"], gated + 1)
                            act.activation(tanhs[:, :, :], below[:, :, :], ACT.Tanh, scale=0.5
                                           ).then_inc(s["tanh_ready"], 1)
                    if r in (2, 3) and may(b):
                        with act.If(b > 0):
                            hidden(pairs + blocks, r - 2)
                    if r == 4 and may(f):
                        with has(act, f):
                            act.wait_ge(s["rstd_ready"], pairs + 1)
                            act.sem_inc(s["act_turn"], 1)
                            for a in range(2):
                                at = 2 * (PAIRS - 1) + a - 2 * pairs
                                q = act.activation(xn2[:, a, :], agg[:, bass.ds(at, 1), 0:C].rearrange("p a b -> p (a b)"),
                                                   ACT.Identity, bias=shift[:, a:a + 1], scale=rstd[:, a:a + 1])
                            q.then_inc(s["xn2_ready"], 1)
                    if r == 5 and may(f):
                        with has(act, f):
                            act.wait_ge(s["pairt_done"], pairs + 1)
                            act.copy(flat(pair_t[:, :, :], "p k t -> p (k t)"), ps_t[:, :]
                                     ).then_inc(s["pairt_copied"], 1)
                    if r in (6, 7) and may(f):
                        with has(act, f):
                            hidden(pairs + blocks + b, r - 6)
                pr.advance(f, b)

            iterations(act, one, END)
            act.wait_ge(s["last_plan"], 1)
            steps = act.value_load(q_n[0:1, 0:1], min_val=1, max_val=QMAX // 2)
            with act.Fori(0, steps) as i:
                for h in range(2):
                    q = 2 * i + h
                    act.wait_ge(s["last_t"], q + 1)
                    act.copy(flat(block_t[:, :, :], "p k t -> p (k t)"), ps_t[:, :]).then_inc(s["last_tc"], 1)
                    for k in range(KH):
                        act.wait_ge(s["last_hid"], KH * q + k + 1)
                        act.activation(hid[:, k, :], ps_h[k % 2][:, 0:BT], ACT.Gelu,
                                       bias=b1_sb[:, k:k + 1]).then_inc(s["last_gelu"], 1)

        @block.vector
        def _(dve):
            turns[id(dve)] = s["dve_turn"]

            def rsqrt(y, v, n):
                a, b, i = nr_a[:, 0:n], nr_b[:, 0:n], nr_i[:, 0:n]
                dve.tensor_scalar(i, v.bitcast(I32), 1, None, ALU.logical_shift_right)
                dve.tensor_scalar(a, v, -0.5, None, ALU.mult)
                dve.drain()
                dve.tensor_scalar(i, i, -1.0, float(0x5F3759DF), ALU.mult, ALU.add)
                dve.drain()
                guess = i.bitcast(F32)
                for step in range(3):
                    old = guess if step == 0 else y
                    dve.tensor_tensor(b, old, old, ALU.mult)
                    dve.drain()
                    dve.tensor_tensor(b, b, a, ALU.mult)
                    dve.drain()
                    dve.scalar_tensor_tensor(y, b, 1.5, old, ALU.add, ALU.mult)
                    dve.drain()

            for n, k in (("split_done", RING), ("block_done", 2), ("sums_final", 1), ("x1_done", 1), ("y_read", 1), ("place_used", 1),
                         ("plan_ready", 1), ("last_read", 2)):
                dve.sem_inc(s[n], k)
            dve.memset(agg[:, NT - 1, :], 0.0)
            dve.memset(dst_i.rearrange("p (j q) -> p j q", q=P)[:, CROWS - 1, :], PAD_DST)
            dve.memset(src_i.rearrange("p (j q) -> p j q", q=P)[:, CROWS - 1, :], 0)
            dve.memset(blk_i.rearrange("p (j q) -> p j q", q=U * P)[:, BROWS - 1, :], PAD_DST)
            dve.drain()
            dve.sem_inc(s["pads_set"], 1)
            dve.memset(src_t[:, NCH:], 0)
            dve.memset(xraw[:, :, :], 0.0)
            dve.memset(ones[:, :], 1.0)
            dve.memset(plan[:, :], 0)

            def layer_norm(g):
                dve.wait_ge(x_in[g], 32 if g == LN_GROUPS - 1 else 16)
                with dve.Fori(0, LT) as t:
                    dve.bn_stats(stats[:, bass.ds(t, 1), :].rearrange("p a b -> p (a b)"),
                                 agg[:, bass.ds(t + g * LT, 1), 0:C].rearrange("p a b -> p (a b)"))
                dve.drain()
                for t in range(LT):
                    dve.bn_aggr(mv[:, t, :], stats[:, t, :])
                dve.drain()
                dve.tensor_scalar(var[:, 0:LT], mv[:, :, 1], EPS, None, ALU.add)
                dve.drain()
                rsqrt(rstd[:, 0:LT], var[:, 0:LT], LT)
                with dve.Fori(0, LT) as t:
                    row = agg[:, bass.ds(t + g * LT, 1), 0:C].rearrange("p a b -> p (a b)")
                    dve.tensor_scalar(row, row, mv[:, bass.ds(t, 1), 0], rstd[:, bass.ds(t, 1)],
                                      ALU.subtract, ALU.mult)
                dve.drain()
                dve.sem_inc(s["normed"], 1)

            layer_norm(0)
            dve.wait_ge(s["edges_in"], 16 * (2 * load_edges(None, dst, None, P) + load_edges(None, dst, None, U * P)))
            dve.tensor_copy(dst_f, dst_i).then_inc(s["dst_float"], 1)
            for g in range(-(-CROWS // 4)):
                m = min(4, CROWS - 4 * g)
                dve.tensor_copy(src_f[g][:, 0:m, :], src_i.rearrange("p (j q) -> p j q", q=P)[:, 4 * g:4 * g + m, :]
                                ).then_inc(s["src_float"], 1)
            bl = blk_i.rearrange("p (j q) -> p j q", q=U * P)
            dve.tensor_reduce(blk_r[:, 0:BROWS], bl, AX.X, ALU.max)
            dve.tensor_reduce(blk_r[:, BROWS:2 * BROWS], bl, AX.X, ALU.min)
            dve.drain()
            dve.tensor_scalar(blk_r, blk_r, P.bit_length() - 1, None, ALU.arith_shift_right)
            dve.drain()
            dve.tensor_copy(blk_f, blk_r)
            dve.drain()
            dve.tensor_scalar(blk_f, blk_f, 0.0, None, ALU.max)
            dve.drain()
            dve.sem_inc(s["blk_float"], 1)
            for j in range(0, CROWS, 4):
                m = min(4 * P, NCH - j * P)
                g = j // 4
                dve.wait_ge(s["tr_done"], 2 * g + 1)
                dve.tensor_copy(dst_t[:, j * P:j * P + m], (ps_t, ps_h[0])[g % 2][:, 0:m]
                                ).then_inc(s["dst_copied"], 1)
            dve.wait_ge(s["blk_tr"], 1)
            dve.tensor_copy(range_f, ps_g[0:2 * BROWS, 0:P])
            dve.drain()
            dve.tensor_copy(range_i, range_f).then_inc(s["blk_rows"], 1)
            for g in range(1, LN_GROUPS):
                layer_norm(g)
            dve.memset(agg[:, :, C], 0.0)
            for h in range(2):
                for u in range(U):
                    dve.tensor_copy(high[:, h, u, C:AW], ones[:, 0:AW - C])
            dve.wait_ge(s["range_in"], 16)
            dve.wait_ge(s["consts_ready"], 9)
            dve.memset(f_a, 0.0)
            dve.memset(f_b, 0.0)
            dve.drain()
            dve.tensor_reduce(f_a[:, 0:ITERS], ranges[0:1, 0:NB].rearrange("o (i r) -> o i r", r=S), AX.X, ALU.max)
            dve.drain()
            old, new = f_a, f_b
            step = 1
            while step < ITERS:
                dve.tensor_tensor(new[:, 0:ITERS], old[:, 0:ITERS], old[:, step:ITERS + step], ALU.max)
                dve.drain()
                old, new = new, old
                step *= 2
            dve.tensor_copy(f_i, old[:, 0:ITERS])
            dve.drain()
            dve.tensor_scalar(f_i, f_i, 1, None, ALU.arith_shift_right)
            dve.drain()
            dve.tensor_copy(old[:, 0:ITERS], f_i)
            dve.drain()
            dve.tensor_scalar(old[:, 0:ITERS], old[:, 0:ITERS], -1.0, float(PAIRS - 1), ALU.mult, ALU.add)
            dve.memset(new[:, 0:ITERS], 1.0)
            dve.drain()
            dve.memset(begun, 0.0)
            dve.drain()
            dve.tensor_tensor_scan(begun[:, 1:ITERS + 1], new[:, 0:ITERS], old[:, 0:ITERS], 0.0, ALU.add, ALU.min)
            dve.drain()
            dve.tensor_tensor(start[:, :], begun[:, 1:ITERS + 1], begun[:, 0:ITERS], ALU.subtract)
            dve.tensor_scalar(pairs_left[:, :], begun[:, ITERS:ITERS + 1], -1.0, float(PAIRS), ALU.mult, ALU.add)
            dve.memset(token_rows[:, :, :], 0.0)
            dve.drain()
            dve.sem_inc(s["tables_ready"], 1)

            pr = Progress(dve)
            added = dve.alloc_register("added")
            tiles = Ranges(dve)
            dve.reg_mov(added, 0)

            def make_onehot(it, r, t):
                at = it * (S * U) + r * U
                q = dve.scalar_tensor_tensor(
                    onehot[:, r % 2, :, :],
                    dst_t[:, bass.ds(at, U)].rearrange("p (u o) -> p u o", o=1).to_broadcast([P, U, P]),
                    tile_base[:, bass.ds(t, 1)],
                    iota[:, :].rearrange("p (o q) -> p o q", o=1).to_broadcast([P, U, P]),
                    ALU.subtract, ALU.is_equal)
                return q

            def prepare(it, r, t):
                make_onehot(it, r, t).then_inc(s["first_ready"], 1)
                dve.wait_ge(s["high_ready"], S * it + r + 1)
                k = (r % RING) * U
                dve.tensor_tensor(low[:, r % 2, :, :], gath[:, k:k + U, :],
                                  high[:, r % 2, :, 0:C].bitcast(F32), ALU.subtract).then_inc(s["split_done"], 1)

            def add_sums(r, t):
                dve.reg_add(added, added, 1)
                n = dve.snap(added)
                dve.wait_ge(s["visit_done"], n)
                row = agg[:, bass.ds(t, 1), :].rearrange("p a b -> p (a b)")
                dve.tensor_tensor(row, row, ps_sum[r % 2][:, 0:C + 1], ALU.add)

            tiles.load(0)
            prepare(0, 0, tiles.first(0))

            def plan_block(i):
                dve.tensor_tensor(avail[:, :], base[0:1, :], nxt[:, :], ALU.subtract)
                dve.drain()
                dve.max(best[:, :], avail[:, :])
                dve.drain()
                dve.max_index(best_at[:, :], best[:, :], avail[:, :])
                dve.tensor_scalar(plan_f[:, 0:1], best[:, 0:1], float(BT), None, ALU.is_ge)
                dve.drain()
                dve.tensor_copy(plan_f[:, 1:2], best_at[:, 0:1])
                dve.drain()
                dve.tensor_scalar(chosen[:, :], iota8[0:1, :], plan_f[:, 1:2], None, ALU.is_equal)
                dve.drain()
                dve.tensor_tensor(avail[:, :], chosen[:, :], nxt[:, :], ALU.mult)
                dve.tensor_scalar(chosen[:, :], chosen[:, :], plan_f[:, 0:1], float(BT), ALU.mult, ALU.mult)
                dve.drain()
                dve.tensor_reduce(plan_f[:, 2:3], avail[:, :], AX.X, ALU.add)
                dve.tensor_tensor(nxt[:, :], nxt[:, :], chosen[:, :], ALU.add)
                dve.drain()
                dve.tensor_copy(plan[:, bass.ds(PW * (i + 1), 3)], plan_f[:, 0:3]).then_inc(s["plan_ready"], 1)

            def store_result(h_rows, h_bd):
                for a in range(2):
                    dve.tensor_tensor(result[:, a, :], ps_m[:, a * C:(a + 1) * C], h_bd, ALU.add)
                dve.tensor_copy(out_at[:, :], h_rows[:, :, ID])
                dve.drain()
                for a in range(2):
                    dve.scalar_tensor_tensor(result[:, a, :], result[:, a, :], h_rows[:, a, PROB:PROB + 1],
                                             h_rows[:, a, C:2 * C], ALU.mult, ALU.add)
                dve.drain()

            def rows_of(pair, a):
                at = 2 * (PAIRS - 1) + a - 2 * pair
                return agg[:, bass.ds(at, 1), 0:C].rearrange("p a b -> p (a b)")

            def norm_of_pair(pairs):
                dve.tensor_scalar(deg[:, :], agg[:, bass.ds(2 * (PAIRS - 1) - 2 * pairs, 2), C], 1.0, None, ALU.max)
                dve.drain()
                rsqrt(norm[:, :], deg[:, :], 2)

            def copy_logits(gated):
                dve.wait_ge(s["gate_done"], gated + 1)
                dve.tensor_scalar(logit_t[:, :], ps_g[0:NE, 0:BT], bg_sb[:, 0:1], None, ALU.add
                                  ).then_inc(s["gate_copied"], 1)

            def pick_experts(gated):
                dve.wait_ge(s["gatet_done"], gated + 1)
                dve.tensor_copy(logit[:, :, :].rearrange("p a e -> p (a e)"), ps_g[:, 256:256 + 2 * NE])
                dve.drain()
                for a in range(2):
                    dve.max(max8[:, a, :], logit[:, a, :])
                dve.drain()
                for a in range(2):
                    dve.max_index(arg8[:, a, :], max8[:, a, :], logit[:, a, :])
                    q = dve.tensor_scalar(below[:, a, :], logit[:, a, :], max8[:, a, 0:1], None, ALU.subtract)
                q.then_inc(s["below_ready"], 1)
                dve.drain()
                dve.tensor_copy(argf[:, :], arg8[:, :, 0])
                dve.drain()
                for a in range(2):
                    q = dve.tensor_scalar(pick[:, a, :], iota8[:, :], argf[:, a:a + 1], None, ALU.is_equal)
                q.then_inc(s["pick_ready"], 1)

            def residual_and_norm(pairs):
                dve.wait_ge(s["x_again"], 32 * pairs + 32)
                dve.wait_ge(s["gnn_done"], pairs + 1)
                for a in range(2):
                    dve.scalar_tensor_tensor(rows_of(pairs, a), ps_w[:, a * C:(a + 1) * C], norm[:, a:a + 1],
                                             xraw[:, a, :], ALU.mult, ALU.add)
                dve.drain()
                dve.sem_inc(s["x1_done"], 1)
                for a in range(2):
                    dve.bn_stats(stats[:, a, :], rows_of(pairs, a))
                dve.drain()
                for a in range(2):
                    dve.bn_aggr(mv[:, a, :], stats[:, a, :])
                dve.drain()
                dve.tensor_scalar(var[:, 0:2], mv[:, 0:2, 1], EPS, None, ALU.add)
                dve.drain()
                rsqrt(rstd[:, 0:2], var[:, 0:2], 2)
                dve.scalar_tensor_tensor(shift[:, :], mv[:, 0:2, 0], -1.0, rstd[:, 0:2], ALU.mult, ALU.mult
                                         ).then_inc(s["rstd_ready"], 1)

            def place_tokens(gated):
                dve.wait_ge(s["tanh_ready"], gated + 1)
                dve.tensor_scalar(expo[:, :, :], tanhs[:, :, :], -1.0, 1.0, ALU.mult, ALU.add)
                dve.wait_ge(s["place_done"], gated + 1)
                dve.tensor_tensor(place[:, 0, :], ps_g[:, 288:288 + NE], base[:, :], ALU.add)
                dve.drain()
                dve.reciprocal(expo[:, :, :], expo[:, :, :])
                dve.tensor_tensor(base[:, :], ps_g[:, 320:320 + NE], base[:, :], ALU.add)
                dve.drain()
                dve.scalar_tensor_tensor(expo[:, :, :], tanhs[:, :, :], 1.0, expo[:, :, :], ALU.add, ALU.mult)
                dve.tensor_tensor(place[:, 1, :], ps_g[:, 288 + NE:288 + 2 * NE], base[:, :], ALU.add)
                dve.drain()
                dve.tensor_tensor(base[:, :], ps_g[:, 320 + NE:320 + 2 * NE], base[:, :], ALU.add)
                dve.tensor_tensor(place[:, :, :], place[:, :, :], pick[:, :, :], ALU.mult)
                dve.tensor_reduce(total[:, :], expo[:, :, :], AX.X, ALU.add)
                dve.drain()
                dve.sem_inc(s["place_used"], 1)
                dve.tensor_reduce(posf[:, :], place[:, :, :], AX.X, ALU.add)
                dve.reciprocal(token_rows[:, :, PROB], total[:, :])
                dve.tensor_copy(token_rows[:, :, ID], node[:, :])
                dve.drain()
                dve.tensor_copy(pos_now[:, :], posf[:, :])
                dve.tensor_scalar(node[:, :], node[:, :], -float(BT), None, ALU.add)
                dve.drain()
                dve.sem_inc(s["pos_ready"], 1)

            def one(i, f, edges, planned=True):
                pairs, gated, blocks = pr.get("pairs", PAIRS - 1), pr.get("gated", PAIRS - 1), pr.get("blocks")
                g = pr.get("g", 1)
                b = block_flag(dve, i) if planned else 0
                if edges:
                    tiles.load(i)
                for r in range(S):
                    if edges:
                        lo, hi = tiles.first(r), tiles.last(r)
                        if r < S - 1:
                            prepare(i, r + 1, tiles.first(r + 1))
                        else:
                            with dve.If(i < ITERS - 1):
                                prepare(i + 1, 0, tiles.first(S))
                        add_sums(r, lo)
                        with dve.If(hi > lo):
                            with dve.Fori(lo + 1, hi + 1) as t:
                                dve.drain()
                                make_onehot(i, r, t).then_inc(s["more_ready"], 1)
                                add_sums(r, t)
                        dve.drain()
                        dve.sem_inc(s["block_done"], 1)
                    if r == 0 and may(f):
                        with has(dve, f):
                            norm_of_pair(pairs)
                    if r == 1:
                        with dve.If(g > 0):
                            copy_logits(gated)
                    if r == 2:
                        with dve.If(g > 0):
                            pick_experts(gated)
                    if r == 3 and may(f):
                        with has(dve, f):
                            residual_and_norm(pairs)
                    if r == 4:
                        with dve.If(g > 0):
                            place_tokens(gated)
                    if r == 5 and may(f):
                        plan_block(i)
                    if r == 6 and may(b):
                        with dve.If(b > 0):
                            dve.wait_ge(s["y_done"], blocks + 1)
                            dve.wait_ge(s["block_in"], 48 * blocks + 48)
                            dve.wait_ge(s["result_free"], blocks + 1)
                            store_result(block_rows, bd_sb[:, :])
                            dve.sem_inc(s["y_read"], 1)
                            dve.sem_inc(s["result_ready"], 1)
                if may(f):
                    dve.sem_inc(s["sums_final"], 1)
                pr.advance(f, b)

            iterations(dve, one, END)

            dve.drain()
            dve.wait_ge(s["rows_free"], PAIRS + 1)
            dve.memset(token_rows[:, :, :], 0.0)
            dve.drain()
            dve.memset(token_rows[:, :, ID], NO_TOKEN)
            dve.tensor_tensor(cnt[:, :], base[0:1, :], nxt[:, :], ALU.subtract)
            dve.tensor_copy(zero_at[:, :], base[0:1, :])
            dve.drain()
            dve.tensor_scalar(cnt_i[:, :], cnt[:, :], float(BT - 1), None, ALU.add)
            dve.drain()
            dve.tensor_scalar(cnt_i[:, :], cnt_i[:, :], BT.bit_length() - 1, None, ALU.arith_shift_right)
            dve.drain()
            dve.tensor_copy(cnt[:, :], cnt_i[:, :])
            dve.memset(cum[:, :], 0.0)
            dve.memset(q_e, 0.0)
            dve.memset(q_row, 0.0)
            dve.drain()
            for e in range(NE):
                dve.tensor_tensor(cum[:, e + 1:e + 2], cum[:, e:e + 1], cnt[:, e:e + 1], ALU.add)
                dve.drain()
            for e in range(NE + 1):
                dve.tensor_scalar(q_lo, q_iota[:, :], cum[:, e:e + 1], None, ALU.is_ge)
                if e < NE:
                    dve.tensor_scalar(q_hi, q_iota[:, :], cum[:, e + 1:e + 2], None, ALU.is_lt)
                    dve.drain()
                    dve.tensor_tensor(q_lo, q_lo, q_hi, ALU.mult)
                dve.drain()
                if e < NE:
                    dve.tensor_scalar(q_hi, q_iota[:, :], cum[:, e:e + 1], float(BT), ALU.subtract, ALU.mult)
                    dve.drain()
                    dve.scalar_tensor_tensor(q_hi, q_hi, nxt[:, e:e + 1], q_lo, ALU.add, ALU.mult)
                else:
                    dve.tensor_scalar(q_hi, q_lo, float(NE * CAP), None, ALU.mult)
                dve.scalar_tensor_tensor(q_e, q_lo, float(min(e, NE - 1)), q_e, ALU.mult, ALU.add)
                dve.drain()
                dve.tensor_tensor(q_row, q_row, q_hi, ALU.add)
                dve.drain()
            dve.tensor_copy(q_tab[:, 0, :], q_e)
            dve.tensor_copy(q_tab[:, 1, :], q_row)
            dve.tensor_scalar(cum[:, NE + 1:NE + 2], cum[:, NE:NE + 1], 1.0, 2.0, ALU.add, ALU.max)
            dve.drain()
            dve.tensor_copy(q_n[:, :], cum[:, NE + 1:NE + 2])
            dve.drain()
            dve.tensor_scalar(q_n[:, :], q_n[:, :], 1, None, ALU.arith_shift_right)
            dve.drain()
            dve.sem_inc(s["last_plan"], 1)
            blocks = pr.get("blocks")
            dve.wait_ge(s["result_free"], blocks + 1)
            dve.sem_inc(s["dve_turn"], 1)
            steps = dve.value_load(q_n[0:1, 0:1], min_val=1, max_val=QMAX // 2)
            with dve.Fori(0, steps) as i:
                for h in range(2):
                    dve.wait_ge(s["last_y"], 2 * i + h + 1)
                    dve.wait_ge(s[f"last_in{h}"], 48 * i + 48)
                    dve.wait_ge(s["last_free"], 2 * i + h + 1)
                    store_result((block_rows, block_rows_2)[h], (bd_sb[:, :], bd_2)[h])
                    dve.sem_inc(s["last_read"], 1)
                    dve.sem_inc(s["last_result"], 1)

        @block.tensor
        def _(pe):
            turns[id(pe)] = s["pe_turn"]
            pe.sem_inc(s["hid_free"], 1)
            pe.wait_ge(s["consts_ready"], 9)
            pe.wait_ge(s["dst_float"], 1)
            pe.wait_ge(s["src_float"], -(-CROWS // 4))
            df = dst_f.rearrange("p (j q) -> p j q", q=P)
            for j in range(0, CROWS, 4):
                g = j // 4
                if g >= 2:
                    pe.wait_ge(s["dst_copied"], g - 1)
                    pe.wait_ge(s["src_copied"], g - 1)
                for f, bank in ((df[:, j:min(j + 4, CROWS), :], (ps_t, ps_h[0])[g % 2]), (src_f[g], (ps_m, ps_h[1])[g % 2])):
                    for k in range(min(4, CROWS - j)):
                        m = min(P, NCH - (j + k) * P)
                        q = pe.transpose(bank[:, k * P:k * P + m], f[0:m, k, :], ident[0:m, 0:m])
                    q.then_inc(s["tr_done"], 1)
            pe.wait_ge(s["blk_float"], 1)
            pe.transpose(ps_g[0:2 * BROWS, 0:P], blk_f, ident[:, :]).then_inc(s["blk_tr"], 1)
            pe.wait_ge(s["tables_ready"], 1)
            pr = Progress(pe)
            more = pe.alloc_register("more")
            pe.reg_mov(more, 0)
            tiles = Ranges(pe)

            def visit(r):
                for u in range(U):
                    halves = [(AW, high), (C, low)]
                    for w, half in halves if u < U - 1 else halves[::-1]:
                        q = pe.matmul(ps_sum[r % 2][:, 0:w], onehot[:, r % 2, u, :], half[:, r % 2, u, :],
                                      start=(u == 0 and half is high), stop=(u == U - 1 and half is high))
                return q

            def sum_block(i, r):
                lo, hi = tiles.first(r), tiles.last(r)
                pe.wait_ge(s["split_done"], S * i + r + 1 + RING)
                pe.sem_inc(s["pe_turn"], 1)
                pe.wait_ge(s["first_ready"], S * i + r + 1)
                visit(r).then_inc(s["visit_done"], 1)
                with pe.If(hi > lo):
                    with pe.Fori(lo + 1, hi + 1):
                        done = pe.snap(more)
                        pe.wait_ge(s["more_ready"], done + 1)
                        visit(r).then_inc(s["visit_done"], 1)
                        pe.reg_add(more, more, 1)

            def hidden(rows_t, gelu, done, index, k0=0, k1=KH):
                for k in range(k0, k1):
                    if k >= 2:
                        pe.wait_ge(s[gelu], KH * index + k - 1)
                    for c in range(KC):
                        q = pe.matmul(ps_h[k % 2][:, 0:BT], w1_sb[:, c, k * P:(k + 1) * P], rows_t[:, c, :],
                                      start=(c == 0), stop=(c == KC - 1))
                    q.then_inc(s[done], 1)

            def transpose_rows(bank, rows):
                for c in range(KC):
                    for a in range(2):
                        q = pe.transpose(bank[:, c * BT + a * P:c * BT + (a + 1) * P], rows[:, a, c * P:(c + 1) * P],
                                         ident[:, :])
                return q

            def expert_product(wd_now, a):
                for k in range(KH):
                    q = pe.matmul(ps_m[:, a * C:(a + 1) * C], hid[:, k, a * P:(a + 1) * P], wd_now[:, k, :],
                                  start=(k == 0), stop=(k == KH - 1))
                return q

            pe.wait_ge(s["weights_in"], 80)

            def one(i, f, edges, planned=True):
                pairs, gated, blocks = pr.get("pairs", PAIRS - 1), pr.get("gated", PAIRS - 1), pr.get("blocks")
                g = pr.get("g", 1)
                b = block_flag(pe, i) if planned else 0
                if edges:
                    tiles.load(i)
                half = KH // 2
                for r in range(S):
                    if edges:
                        sum_block(i, r)
                    if r == 0:
                        with pe.If(g > 0):
                            pe.wait_ge(s["gelu_done"], KH * pairs + KH * blocks)
                            pe.wait_ge(s["place_used"], gated + 1)
                            for k in range(KH):
                                q = pe.matmul(ps_g[0:NE, 0:BT], wg_sb[:, k, :], hid[:, k, :],
                                              start=(k == 0), stop=(k == KH - 1))
                            q.then_inc(s["gate_done"], 1)
                            pe.wait_ge(s["gate_done"], gated + 1)
                            pe.sem_inc(s["hid_free"], 1)
                    if r == 1:
                        if may(f):
                            with has(pe, f):
                                pe.wait_ge(s["scaled_ready"], pairs + 1)
                                transpose_rows(ps_t, scaled).then_inc(s["scaledt_done"], 1)
                        if may(b):
                            with pe.If(b > 0):
                                pe.wait_ge(s["block_in"], 48 * blocks + 48)
                                pe.wait_ge(s["gelu_done"], KH * pairs + KH * blocks)
                                transpose_rows(ps_h[0], block_rows).then_inc(s["blockt_done"], 1)
                    if r == 2:
                        with pe.If(g > 0):
                            pe.wait_ge(s["gate_copied"], gated + 1)
                            pe.sem_inc(s["pe_turn"], 1)
                            for a in range(2):
                                q = pe.transpose(ps_g[:, 256 + a * NE:256 + (a + 1) * NE], logit_t[:, a * P:(a + 1) * P],
                                                 ident[0:NE, 0:NE])
                            q.then_inc(s["gatet_done"], 1)
                        if may(f):
                            with has(pe, f):
                                pe.wait_ge(s["x1_done"], pairs + 1)
                                pe.wait_ge(s["scaledt_copied"], pairs + 1)
                                for a in range(2):
                                    for c in range(KC):
                                        q = pe.matmul(ps_w[:, a * C:(a + 1) * C], pair_t[:, c, a * P:(a + 1) * P],
                                                      w_sb[:, c, :], start=(c == 0), stop=(c == KC - 1))
                                q.then_inc(s["gnn_done"], 1)
                    if r in (2, 3, 4) and may(b):
                        with pe.If(b > 0):
                            if r == 2:
                                pe.wait_ge(s["blockt_copied"], blocks + 1)
                                hidden(block_t, "gelu_done", "hid_done", pairs + blocks, 0, half)
                            if r == 3:
                                hidden(block_t, "gelu_done", "hid_done", pairs + blocks, half, KH)
                            if r == 4:
                                pe.wait_ge(s["gelu_done"], KH * pairs + KH * blocks + KH)
                                pe.wait_ge(s["y_read"], blocks + 1)
                                expert_product(wd_sb, 0)
                    if r == 3:
                        with pe.If(g > 0):
                            pe.wait_ge(s["pick_ready"], gated + 1)
                            both = pick[:, :, :].rearrange("p a e -> p (a e)")
                            pe.matmul(ps_g[:, 288:288 + 2 * NE], before[:, :], both, start=True, stop=True)
                            pe.matmul(ps_g[:, 320:320 + 2 * NE], ones[:, :], both, start=True, stop=True
                                      ).then_inc(s["place_done"], 1)
                    if r == 5:
                        if may(f):
                            with has(pe, f):
                                pe.wait_ge(s["xn2_ready"], pairs + 1)
                                transpose_rows(ps_t, xn2).then_inc(s["pairt_done"], 1)
                        if may(b):
                            with pe.If(b > 0):
                                expert_product(wd_sb, 1).then_inc(s["y_done"], 1)
                                pe.wait_ge(s["y_done"], blocks + 1)
                                pe.sem_inc(s["hid_free"], 1)
                    if r in (6, 7) and may(f):
                        with has(pe, f):
                            if r == 6:
                                pe.wait_ge(s["pairt_copied"], pairs + 1)
                            hidden(pair_t, "gelu_done", "hid_done", pairs + blocks + b, (r - 6) * half, (r - 5) * half)
                pr.advance(f, b)

            iterations(pe, one, END)
            pe.wait_ge(s["last_plan"], 1)
            steps = pe.value_load(q_n[0:1, 0:1], min_val=1, max_val=QMAX // 2)
            with pe.Fori(0, steps) as i:
                for h in range(2):
                    q = 2 * i + h
                    rows, wd_now = ((block_rows[:, :, :], wd_sb[:, :, :]), (block_rows_2, wd_2))[h]
                    pe.wait_ge(s[f"last_in{h}"], 48 * i + 48)
                    transpose_rows(ps_t, rows).then_inc(s["last_t"], 1)
                    pe.wait_ge(s["last_tc"], q + 1)
                    hidden(block_t, "last_gelu", "last_hid", q)
                    pe.wait_ge(s["last_gelu"], KH * q + KH)
                    pe.wait_ge(s["last_read"], q + 2)
                    expert_product(wd_now, 0)
                    expert_product(wd_now, 1).then_inc(s["last_y"], 1)


def kernel(x, src, dst, L0_gnn_weight, L0_ffn_W1, L0_ffn_b1, L0_ffn_Wg, L0_ffn_bg, L0_ffn_Wd, L0_ffn_bd):
    import numpy as np
    import concourse.bacc as bacc
    from concourse.bass_utils import run_bass_kernel_spmd

    nc = bacc.Bacc("TRN2", target_bir_lowering=False, num_devices=1)
    arrays, args = {}, []
    for name, a in (("x", x), ("src", src), ("dst", dst), ("w_gnn", L0_gnn_weight), ("w1", L0_ffn_W1),
                    ("b1", L0_ffn_b1), ("wg", L0_ffn_Wg), ("bg", L0_ffn_bg), ("wd", L0_ffn_Wd), ("bd", L0_ffn_bd)):
        a = np.ascontiguousarray(a[::-1] if name in ("src", "dst") else a)
        arrays[name] = a
        args.append(nc.dram_tensor(name, a.shape, mybir.dt.from_np(a.dtype), kind="ExternalInput").ap())
    out = nc.dram_tensor("out", x.shape, mybir.dt.float32, kind="ExternalOutput").ap()
    gnn_moe_program(nc, *args, out)
    r = run_bass_kernel_spmd(nc, [arrays], core_ids=[0])
    return r.results[0]["out"]
```
